# Optimizing a Trainium2 kernel written in Bass

```python
import numpy as np
import jax
import jax.numpy as jnp

def _softmax(x, axis=-1):
    return jax.nn.softmax(x, axis=axis)

def _gelu(x):
    return jax.nn.gelu(x, approximate=True)

def _silu(x):
    return jax.nn.silu(x)

def _sigmoid(x):
    return jax.nn.sigmoid(x)

def _layernorm(x, axis=-1, eps=1e-05):
    m = jnp.mean(x, axis=axis, keepdims=True)
    v = jnp.var(x, axis=axis, keepdims=True)
    return (x - m) / jnp.sqrt(v + eps)

def _scatter_add(tgt, idx, src, axis=0):
    return tgt.at[idx].add(src)

def _segment_sum(src, seg, n):
    return jax.ops.segment_sum(src, seg, n)
kernel_name = 'mk_adaln_ffn_d1_seqx_r8_b09360'

def setup_inputs(seed: int=0):
    np.random.seed(seed)
    _w = jnp.asarray

    def _rec_inputs():
        import jax
        import jax.numpy as jnp
        _rk = jax.random.key(seed)
        x = -8.015e-05 + 0.9999 * jax.random.normal(jax.random.fold_in(_rk, 1), (4, 256, 256), jnp.float32)
        _lenS = 256 - jax.random.randint(jax.random.fold_in(_rk, 7), (4,), 0, max(1, 256 // 4) + 1, jnp.int32)
        _lenS2 = 256 - jax.random.randint(jax.random.fold_in(_rk, 8), (4,), 0, max(1, 256 // 4) + 1, jnp.int32)
        cond_1024 = 0.00191187 + 0.999416 * jax.random.normal(jax.random.fold_in(_rk, 11), (4, 128), jnp.float32)
        return (x, cond_1024)
    x, cond_1024 = _rec_inputs()

    def _L0_cond_setup():
        import jax, jax.numpy as jnp
        import numpy as np
        B, N, V_DIM, Q_DIM = (32, 100, 256, 128)
        key = jax.random.key(seed)
        k1, k2, k3, k4 = jax.random.split(key, 4)
        v = jax.random.normal(k1, (B, N, V_DIM), dtype=jnp.float32)
        q = jax.random.normal(k2, (B, Q_DIM), dtype=jnp.float32)
        W3 = jax.random.normal(k3, (Q_DIM, V_DIM), dtype=jnp.float32) * (1.0 / np.sqrt(Q_DIM))
        b3 = jnp.zeros((V_DIM,), dtype=jnp.float32)
        W2 = jax.random.normal(k4, (V_DIM, V_DIM), dtype=jnp.float32) * (1.0 / np.sqrt(V_DIM))
        b2 = jnp.zeros((V_DIM,), dtype=jnp.float32)
        return {'v': v, 'q': q, 'W3': W3, 'b3': b3, 'W2': W2, 'b2': b2}
    _L0_cond_all = _L0_cond_setup()
    _L0_cond_in = {k: v for k, v in _L0_cond_all.items() if k in ('W3', 'b3', 'W2', 'b2')}
    del _L0_cond_all

    def _L0_ffn_setup():
        import jax, jax.numpy as jnp
        import numpy as np
        EPS = 1e-05
        ROPE_BASE = 150000.0
        NHEADS = 32
        KVHEADS = 8
        HEAD_DIM = 64
        TOP_K = 4

        def _rms(x, w):
            return x * jax.lax.rsqrt(jnp.mean(x * x, -1, keepdims=True) + EPS) * w

        def _rope(q, k):
            S, hd = (q.shape[1], q.shape[-1])
            half = hd // 2
            inv = 1.0 / ROPE_BASE ** (jnp.arange(half, dtype=jnp.float32) / half)
            ang = jnp.arange(S, dtype=jnp.float32)[:, None] * inv
            cos = jnp.concatenate([jnp.cos(ang), jnp.cos(ang)], -1)[None, :, None, :]
            sin = jnp.concatenate([jnp.sin(ang), jnp.sin(ang)], -1)[None, :, None, :]

            def rot(t):
                t1, t2 = (t[..., :half], t[..., half:])
                return jnp.concatenate([-t2, t1], -1)
            return (q * cos + rot(q) * sin, k * cos + rot(k) * sin)
        key = jax.random.key(seed)
        ks = jax.random.split(key, 12)
        B, S, D, H, E = (1, 128, 256, 256, 16)
        s = 0.02
        return {'x': jax.random.normal(ks[0], (B, S, D), jnp.float32), 'ln_w': jnp.ones((D,), jnp.float32), 'ff_ln_w': jnp.ones((D,), jnp.float32), 'wq': jax.random.normal(ks[1], (D, NHEADS * HEAD_DIM), jnp.float32) * s, 'wk': jax.random.normal(ks[2], (D, KVHEADS * HEAD_DIM), jnp.float32) * s, 'wv': jax.random.normal(ks[3], (D, KVHEADS * HEAD_DIM), jnp.float32) * s, 'wo': jax.random.normal(ks[4], (NHEADS * HEAD_DIM, D), jnp.float32) * s, 'wg': jax.random.normal(ks[5], (D, E), jnp.float32) * s, 'w1': jax.random.normal(ks[6], (E, D, H), jnp.float32) * s, 'w3': jax.random.normal(ks[7], (E, D, H), jnp.float32) * s, 'w2': jax.random.normal(ks[8], (E, H, D), jnp.float32) * s}
    _L0_ffn_all = _L0_ffn_setup()
    _L0_ffn_in = {k: v for k, v in _L0_ffn_all.items() if k in ('ln_w', 'ff_ln_w', 'wq', 'wk', 'wv', 'wo', 'wg', 'w1', 'w3', 'w2')}
    del _L0_ffn_all
    return {'x': x, 'cond_1024': cond_1024, 'L0_cond_W3': _L0_cond_in['W3'], 'L0_cond_b3': _L0_cond_in['b3'], 'L0_cond_W2': _L0_cond_in['W2'], 'L0_cond_b2': _L0_cond_in['b2'], 'L0_ffn_ln_w': _L0_ffn_in['ln_w'], 'L0_ffn_ff_ln_w': _L0_ffn_in['ff_ln_w'], 'L0_ffn_wq': _L0_ffn_in['wq'], 'L0_ffn_wk': _L0_ffn_in['wk'], 'L0_ffn_wv': _L0_ffn_in['wv'], 'L0_ffn_wo': _L0_ffn_in['wo'], 'L0_ffn_wg': _L0_ffn_in['wg'], 'L0_ffn_w1': _L0_ffn_in['w1'], 'L0_ffn_w3': _L0_ffn_in['w3'], 'L0_ffn_w2': _L0_ffn_in['w2']}

def reference(x, cond_1024, L0_cond_W3, L0_cond_b3, L0_cond_W2, L0_cond_b2, L0_ffn_ln_w, L0_ffn_ff_ln_w, L0_ffn_wq, L0_ffn_wk, L0_ffn_wv, L0_ffn_wo, L0_ffn_wg, L0_ffn_w1, L0_ffn_w3, L0_ffn_w2):
    import jax
    import jax.numpy as jnp

    def _L0_cond_ref(v, q, W3, b3, W2, b2):
        import jax, jax.numpy as jnp
        import numpy as np
        B, N, V_DIM, Q_DIM = (32, 100, 256, 128)
        q_emb = jax.nn.relu(q @ W3 + b3)
        n = v.shape[1]
        v_sum = jnp.sum(v, axis=1, keepdims=True)
        x = (n * v + v_sum) * q_emb[:, None, :]
        return jax.nn.relu(x @ W2 + b2)

    def _L0_ffn_ref(x, ln_w, ff_ln_w, wq, wk, wv, wo, wg, w1, w3, w2):
        import jax, jax.numpy as jnp
        import numpy as np
        EPS = 1e-05
        ROPE_BASE = 150000.0
        NHEADS = 32
        KVHEADS = 8
        HEAD_DIM = 64
        TOP_K = 4

        def _rms(x, w):
            return x * jax.lax.rsqrt(jnp.mean(x * x, -1, keepdims=True) + EPS) * w

        def _rope(q, k):
            S, hd = (q.shape[1], q.shape[-1])
            half = hd // 2
            inv = 1.0 / ROPE_BASE ** (jnp.arange(half, dtype=jnp.float32) / half)
            ang = jnp.arange(S, dtype=jnp.float32)[:, None] * inv
            cos = jnp.concatenate([jnp.cos(ang), jnp.cos(ang)], -1)[None, :, None, :]
            sin = jnp.concatenate([jnp.sin(ang), jnp.sin(ang)], -1)[None, :, None, :]

            def rot(t):
                t1, t2 = (t[..., :half], t[..., half:])
                return jnp.concatenate([-t2, t1], -1)
            return (q * cos + rot(q) * sin, k * cos + rot(k) * sin)
        B, S, D = x.shape
        h = _rms(x, ln_w)
        q = (h @ wq).reshape(B, S, NHEADS, HEAD_DIM)
        k = (h @ wk).reshape(B, S, KVHEADS, HEAD_DIM)
        v = (h @ wv).reshape(B, S, KVHEADS, HEAD_DIM)
        q, k = _rope(q, k)
        g = NHEADS // KVHEADS
        k = jnp.repeat(k, g, axis=2)
        v = jnp.repeat(v, g, axis=2)
        scores = jnp.einsum('bqhd,bkhd->bhqk', q, k) / np.float32(np.sqrt(HEAD_DIM))
        causal = jnp.tril(jnp.ones((S, S), bool))
        scores = jnp.where(causal[None, None], scores, jnp.float32(-1e+30))
        attn = jax.nn.softmax(scores, -1)
        o = jnp.einsum('bhqk,bkhd->bqhd', attn, v).reshape(B, S, NHEADS * HEAD_DIM)
        x = x + o @ wo
        h = _rms(x, ff_ln_w)
        logits = h @ wg
        topv, topi = jax.lax.top_k(logits, TOP_K)
        gate = jax.nn.softmax(topv, -1)
        bidx = jnp.arange(B)[:, None, None]
        sidx = jnp.arange(S)[None, :, None]
        weights = jnp.zeros_like(logits).at[bidx, sidx, topi].set(gate)
        a = jax.nn.silu(jnp.einsum('bsd,edh->bseh', h, w1)) * jnp.einsum('bsd,edh->bseh', h, w3)
        y = jnp.einsum('bseh,ehd->bsed', a, w2)
        moe = jnp.einsum('bsed,bse->bsd', y, weights)
        return x + moe
    x = x + _L0_ffn_ref(_L0_cond_ref(x, cond_1024, L0_cond_W3, L0_cond_b3, L0_cond_W2, L0_cond_b2), L0_ffn_ln_w, L0_ffn_ff_ln_w, L0_ffn_wq, L0_ffn_wk, L0_ffn_wv, L0_ffn_wo, L0_ffn_wg, L0_ffn_w1, L0_ffn_w3, L0_ffn_w2)
    return x

_drawn_inputs = setup_inputs


def setup_inputs(seed=0):
    import zlib

    import numpy as np

    out = dict(_drawn_inputs(seed))
    spreads = {'L0_cond_b3': (0.0, 0.1),
     'L0_cond_b2': (0.0, 0.8),
     'L0_ffn_ln_w': (1.0, 0.6),
     'L0_ffn_ff_ln_w': (1.0, 0.6)}
    factors = {'L0_ffn_wq': 8.0,
     'L0_ffn_wk': 8.0,
     'L0_ffn_wv': 8.0,
     'L0_ffn_wo': 8.0,
     'L0_ffn_wg': 8.0,
     'L0_ffn_w1': 8.0,
     'L0_ffn_w3': 8.0,
     'L0_ffn_w2': 8.0}
    for name, (base, spread) in spreads.items():
        noise = np.random.default_rng([zlib.crc32(name.encode()), seed]).standard_normal(out[name].shape)
        drawn = base * np.exp(spread * noise) if base else spread * noise
        out[name] = jnp.asarray(drawn.astype(out[name].dtype))
    for name, factor in factors.items():
        out[name] = (out[name] * factor).astype(out[name].dtype)
    return out
```

```python
from contextlib import ExitStack

import numpy as np
import concourse.bass as bass
from concourse import mybir
from concourse.alu_op_type import AluOpType as ALU

F32 = mybir.dt.float32
F32R = mybir.dt.float32r
BF16 = mybir.dt.bfloat16
ACT = mybir.ActivationFunctionType
X = mybir.AxisListType.X

P = 128
B, S, D = 4, 256, 256
NT = B * S // P
KD = D // P
HEADS, KV, HD = 32, 8, 64
GH = HEADS // KV
E, TOPK = 16, 4
EPS = 1e-5
QKV = GH * HD + 2 * HD
ROT = (GH + 1) * HD
WQ, WO = KD * QKV, 2 * D
EW = 3 * KD * D
BIG = 3.0e38
SMALL = dict(cond=0, b3=4, ln=6, ffln=8, wg=10, ident=42)
NSMALL = 170


def build(nc, small, w3, w2c, b2, xT, xn, rope, mask, attw, expw, out):
    with ExitStack() as outer:
        def sem(name):
            return outer.enter_context(nc.semaphore(name))

        def keep(name, shape, dt=F32):
            return outer.enter_context(nc.sbuf_tensor(name, shape, dt))

        sm = keep("sm", [P, NSMALL])
        ident = sm[:, SMALL["ident"]:SMALL["ident"] + P]
        ident_bf = keep("ident_bf", [P, P], BF16)
        mask_sb = keep("mask_sb", [P, P], BF16)
        ones = keep("ones", [P, P])
        y = keep("y", [P, NT, D])
        actT_hi = keep("actT_hi", [P, KD, B * S], F32R)
        actT_lo = keep("actT_lo", [P, KD, B * S], F32R)
        ss = keep("ss", [P, 2, NT])
        var = keep("var", [P, 2, NT])
        rstd = keep("rstd", [P, 2, NT])
        nt1 = keep("nt1", [P, 2, NT])
        hn = keep("hn", [P, 2, 2, D])
        junk = keep("junk", [P, 2, D])
        exp_raw = keep("exp_raw", [P, 2, EW])
        wg_hi = keep("wg_hi", [P, KD, E], F32R)
        wg_lo = keep("wg_lo", [P, KD, E], F32R)
        gates = keep("gates", [P, NT, E])
        psum = outer.enter_context(nc.psum_tensor("psum", [P, 8, 512], F32))

        with ExitStack() as att:
            def tmp(name, shape, dt=F32):
                return att.enter_context(nc.sbuf_tensor(name, shape, dt))

            hT_hi = tmp("hT_hi", [P, KD, B * S], F32R)
            hT_lo = tmp("hT_lo", [P, KD, B * S], F32R)
            att_raw = tmp("att_raw", [P, WQ + WO])
            att_hi = tmp("att_hi", [P, 2, WQ + WO], F32R)
            att_lo = tmp("att_lo", [P, 2, WQ + WO], F32R)
            rope_sb = tmp("rope_sb", [P, 2, 2, ROT])
            xTs = tmp("xTs", [P, KD, B * S])
            xa = tmp("xa", [P, KD, B * S])
            w3_sb = tmp("w3_sb", [P, D])
            w2_raw = tmp("w2_raw", [P, KD, D])
            w2_hi = tmp("w2_hi", [P, KD, D], F32R)
            w2_lo = tmp("w2_lo", [P, KD, D], F32R)
            b2_sb = tmp("b2_sb", [1, 2, D])
            vsum = tmp("vsum", [P, B, KD])
            qemb = tmp("qemb", [P, KD, B])
            rc = tmp("rc", [P, 2, ROT])
            rs_ = tmp("rs_", [P, 2, ROT])
            rot = tmp("rot", [P, 2, ROT + HD])
            qT_hi = tmp("qT_hi", [P, 2, S], F32R)
            qT_lo = tmp("qT_lo", [P, 2, S], F32R)
            kT_hi = tmp("kT_hi", [P, S], F32R)
            kT_lo = tmp("kT_lo", [P, S], F32R)
            v_hi = tmp("v_hi", [P, B, 2, 3 * HD], F32R)
            v_lo = tmp("v_lo", [P, B, 2, 3 * HD], F32R)
            prob = tmp("prob", [P, 2, 2, 3 * P])
            pT_hi = tmp("pT_hi", [P, 2, 2, 3 * P], F32R)
            pT_lo = tmp("pT_lo", [P, 2, 2, 3 * P], F32R)
            nmax = tmp("nmax", [P, 2, 2, 2])
            rsum = tmp("rsum", [P, 2, 2, 2])
            rinv = tmp("rinv", [P, 2, 2, 2])
            oT_hi = tmp("oT_hi", [P, 2, 2, S], F32R)
            oT_lo = tmp("oT_lo", [P, 2, 2, S], F32R)

        with ExitStack() as moe:
            def etmp(name, shape, dt=F32):
                return moe.enter_context(nc.sbuf_tensor(name, shape, dt))

            exp_hi = etmp("exp_hi", [P, 2, EW], F32R)
            exp_lo = etmp("exp_lo", [P, 2, EW], F32R)
            sil = etmp("sil", [P, 2, 512])
            prod = etmp("prod", [P, 2, 512])
            aT_hi = etmp("aT_hi", [P, 2, 2, 512], F32R)
            aT_lo = etmp("aT_lo", [P, 2, 2, 512], F32R)
            x_sb = etmp("x_sb", [P, NT, D])
            logit = etmp("logit", [P, NT, E + 4])
            top = etmp("top", [P, NT, 8])
            left = etmp("left", [P, NT, E + 4])
            chosen = etmp("chosen", [P, NT, E])
            expl = etmp("expl", [P, NT, E])
            gsum = etmp("gsum", [P, NT])

        small_in = sem("small_in")
        cond_in = sem("cond_in")
        w2_in = sem("w2_in")
        x_in = [sem(f"x_in{b}") for b in range(B)]
        rope_in = sem("rope_in")
        mask_in = sem("mask_in")
        attw_in = sem("attw_in")
        expw_in = [sem("expw_in0"), sem("expw_in1")]
        xn_in = sem("xn_in")
        stored = sem("stored")
        consts_set = sem("consts_set")
        zeros_set = sem("zeros_set")
        qemb_ps = sem("qemb_ps")
        pre_dve = sem("pre_dve")
        w2h_set = sem("w2h_set")
        w2_split = sem("w2_split")
        pre_pool = sem("pre_pool")
        xq_scaled = sem("xq_scaled")
        xqh_set = sem("xqh_set")
        xql_set = sem("xql_set")
        cond_ps = sem("cond_ps")
        y_set = sem("y_set")
        sq_set = sem("sq_set")
        var_set = sem("var_set")
        std_set = sem("std_set")
        hn_set = sem("hn_set")
        hnT_ps = sem("hnT_ps")
        hh_set = sem("hh_set")
        hl_set = sem("hl_set")
        attw_split = sem("attw_split")
        attwo_split = sem("attwo_split")
        atth_set = sem("atth_set")
        proj_ps = sem("proj_ps")
        rope_mul = sem("rope_mul")
        vh_set = sem("vh_set")
        vl_set = sem("vl_set")
        rope_add = sem("rope_add")
        qkT_ps = sem("qkT_ps")
        qkh_set = sem("qkh_set")
        qkl_set = sem("qkl_set")
        score_ps = sem("score_ps")
        max_set = sem("max_set")
        exp_set = sem("exp_set")
        inv_set = sem("inv_set")
        norm_set = sem("norm_set")
        pT_ps = sem("pT_ps")
        pTh_set = sem("pTh_set")
        pTl_set = sem("pTl_set")
        pv_ps = sem("pv_ps")
        oh_set = sem("oh_set")
        ol_set = sem("ol_set")
        wo_ps = sem("wo_ps")
        x1_set = sem("x1_set")
        logit_ps = sem("logit_ps")
        logit_set = sem("logit_set")
        lshift = sem("lshift")
        lexp = sem("lexp")
        expw_split = sem("expw_split")
        exph_set = sem("exph_set")
        up1_ps = sem("up1_ps")
        up3_ps = sem("up3_ps")
        sil_set = sem("sil_set")
        prod_set = sem("prod_set")
        ah_set = sem("ah_set")
        al_set = sem("al_set")
        down_ps = sem("down_ps")
        acc_set = sem("acc_set")

        block = outer.enter_context(nc.Block())

        PJ, QO, PV = 4, 6, 7
        S_BANK, PT_BANK = 0, 2
        LAST = 4 * KV - 1

        def before(g, b):
            return (g, b - 1) if b else (g - 1, B - 1)

        def after(g, b):
            return (g, b + 1) if b < B - 1 else (g + 1, 0)

        def run_steps(eng, step):
            for b in range(B):
                step(0, b, b >= 1, b >= 2, True)
            with eng.Fori(1, KV - 1) as g:
                for b in range(B):
                    step(g, b, True, True, True)
            for b in range(B):
                step(KV - 1, b, True, True, b < B - 1)

        def wait(eng, s, count):
            if not isinstance(count, int) or count > 0:
                eng.wait_ge(s, count)

        @block.sync
        def _(sp):
            sp.dma_start(sm[:, :], small).then_inc(small_in, 16)
            sp.dma_start(w3_sb[:, :], w3).then_inc(cond_in, 16)
            xv = xT.rearrange("(k p) (b s) -> b p k s", p=P, b=B)
            for b in range(B):
                sp.dma_start(xTs[:, :, b * S:(b + 1) * S], xv[b]).then_inc(x_in[b], 16)
                if b == 0:
                    sp.dma_start(w2_raw[:, :, :], w2c.rearrange("(k p) n -> p k n", p=P)).then_inc(w2_in, 16)
                    sp.dma_start(b2_sb[:, 0, :], b2).then_inc(cond_in, 16)
                    sp.dma_start(b2_sb[:, 1, :], b2).then_inc(cond_in, 16)
            sp.dma_start(att_raw[:, :], attw[0]).then_inc(attw_in, 16)
            sp.dma_start(rope_sb[:, :, :, :], rope).then_inc(rope_in, 16)
            sp.dma_start(mask_sb[:, :], mask).then_inc(mask_in, 16)
            for e in range(2):
                sp.dma_start(exp_raw[:, e, :], expw[e]).then_inc(expw_in[e], 16)
            with sp.Fori(1, KV) as g:
                sp.wait_ge(attwo_split, g)
                sp.dma_start(att_raw[:, :], attw[g]).then_inc(attw_in, 16)
            sp.wait_ge(wo_ps, 4 * KV)
            sp.wait_ge(x1_set, 4 * KV)
            sp.dma_start(x_sb[:, :, :], xn.rearrange("(t p) d -> p t d", p=P)).then_inc(xn_in, 16)
            with sp.Fori(1, E // 2) as ep:
                for par in range(2):
                    sp.wait_ge(expw_split, 2 * ep + par - 1)
                    sp.dma_start(exp_raw[:, par, :], expw[2 * ep + par]).then_inc(expw_in[par], 16)
            ov = out.rearrange("(t p) d -> p t d", p=P)
            for c in range(4):
                sp.wait_ge(acc_set, 4 * (E - 1) + c + 1)
                sp.dma_start(ov[:, 2 * c:2 * c + 2, :], y[:, 2 * c:2 * c + 2, :]).then_inc(stored, 16)
            sp.wait_ge(stored, 64)

        @block.tensor
        def _(pe):
            def three(out_ap, sh, sl, mh, ml, start, stop):
                pe.matmul(out_ap, sh, mh, start=start, stop=False)
                pe.matmul(out_ap, sh, ml, start=False, stop=False)
                return pe.matmul(out_ap, sl, mh, start=False, stop=stop)

            pe.wait_ge(small_in, 16)
            pe.wait_ge(cond_in, 48)
            for k in range(KD):
                mm = pe.matmul(psum[:, 4, k * B:(k + 1) * B], w3_sb[:, k * P:(k + 1) * P],
                               sm[:, 0:B], start=True, stop=True)
            mm.then_inc(qemb_ps, 1)
            pe.wait_ge(w2_split, 1)
            pe.wait_ge(consts_set, 1)
            pe.wait_ge(zeros_set, 1)
            for b in range(B):
                pe.matmul(psum[:, b, :], ones[0:1, :], b2_sb[:, :, :].rearrange("p a d -> p (a d)"),
                          start=True, stop=False)
                pe.wait_ge(xql_set, b + 1)
                for t in range(2):
                    tok = slice(b * S + t * P, b * S + (t + 1) * P)
                    for k in range(KD):
                        mm = three(psum[:, b, t * D:(t + 1) * D], actT_hi[:, k, tok], actT_lo[:, k, tok],
                                   w2_hi[:, k, :], w2_lo[:, k, :], False, t == 1 and k == KD - 1)
                mm.then_inc(cond_ps, 1)

            def norm_T(n):
                b = n % B
                pe.wait_ge(hn_set, n + 1)
                for k in range(KD):
                    for t in range(2):
                        mm = pe.transpose(psum[:, 4 + b, k * S + t * P:k * S + (t + 1) * P],
                                          hn[:, n % 2, t, k * P:(k + 1) * P], ident)
                mm.then_inc(hnT_ps, 1)

            for n in range(B):
                norm_T(n)

            def proj(g, b, t):
                i = 4 * g + b
                if t == 0:
                    pe.wait_ge(attw_split, g + 1)
                    wait(pe, qkl_set, i)
                else:
                    wait(pe, vl_set, 2 * i)
                if isinstance(g, int) and g == 0:
                    pe.wait_ge(hl_set, B if b == 0 else b + 1)
                tok = slice(b * S + t * P, b * S + (t + 1) * P)
                for k in range(KD):
                    w = slice(k * QKV, (k + 1) * QKV)
                    mm = three(psum[:, PJ + t, 0:QKV], hT_hi[:, k, tok], hT_lo[:, k, tok],
                               att_hi[:, g % 2, w], att_lo[:, g % 2, w], k == 0, k == KD - 1)
                mm.then_inc(proj_ps, 1)

            def qkT(g, b):
                i = 4 * g + b
                pe.wait_ge(rope_add, i + 1)
                pe.wait_ge(vl_set, 2 * i + 2)
                wait(pe, x1_set, i - 3)
                for p in range(2):
                    for t in range(2):
                        pe.transpose(psum[:, QO, p * S + t * P:p * S + (t + 1) * P],
                                     rot[:, t, p * P:(p + 1) * P], ident)
                for t in range(2):
                    mm = pe.transpose(psum[:, PJ, t * P:(t + 1) * P], rot[:, t, 2 * P:3 * P], ident)
                mm.then_inc(qkT_ps, 1)

            def scores(g, b, p):
                i = 4 * g + b
                m = 2 * i + p
                pe.wait_ge(qkl_set, i + 1)
                wait(pe, exp_set, m)
                if isinstance(g, int) and g == 0 and b == 0 and p == 0:
                    pe.wait_ge(mask_in, 16)
                for t in range(2):
                    keys, cols = slice(0, (t + 1) * P), slice(t * P, t * P + (t + 1) * P)
                    q = slice(t * P, (t + 1) * P)
                    for n, (qs, ks) in enumerate(((qT_hi, kT_hi), (qT_hi, kT_lo), (qT_lo, kT_hi))):
                        for h in range(2):
                            r = slice(h * HD, (h + 1) * HD)
                            pe.matmul(psum[:, S_BANK + h, cols], qs[r, p, q], ks[r, keys],
                                      start=n == 0, stop=False)
                    for h in range(2):
                        mm = pe.matmul(psum[:, S_BANK + h, 2 * t * P:(2 * t + 1) * P], ident_bf[:, :],
                                       mask_sb[:, :], start=False, stop=True)
                mm.then_inc(score_ps, 1)

            def probT(g, b, p):
                m = 2 * (4 * g + b) + p
                pe.wait_ge(norm_set, m + 1)
                wait(pe, pTl_set, m)
                for h in range(2):
                    for blk in range(3):
                        mm = pe.transpose(psum[:, PT_BANK + h, blk * P:(blk + 1) * P],
                                          prob[:, p, h, blk * P:(blk + 1) * P], ident)
                mm.then_inc(pT_ps, 1)

            def value(g, b, p):
                m = 2 * (4 * g + b) + p
                pe.wait_ge(pTl_set, m + 1)
                wait(pe, ol_set, m)
                for h in range(2):
                    v = slice((1 - h) * HD, (1 - h) * HD + P)
                    for kt in range(2):
                        q = slice(kt * P, S)
                        pt = slice(2 * kt * P, 2 * kt * P + S - kt * P)
                        mm = three(psum[:, PV, q], v_hi[:, b, kt, v], v_lo[:, b, kt, v],
                                   pT_hi[:, p, h, pt], pT_lo[:, p, h, pt],
                                   h == 0 and kt == 0, h == 1 and kt == 1)
                mm.then_inc(pv_ps, 1)

            def output(g, b, later):
                i = 4 * g + b
                pe.wait_ge(ol_set, 2 * i + 2)
                pe.wait_ge(attwo_split, g + 1)
                wait(pe, x1_set, i)
                pe.wait_ge(qkl_set, later)
                for t in range(2):
                    q = slice(t * P, (t + 1) * P)
                    for p in range(2):
                        w = slice(WQ + p * D, WQ + (p + 1) * D)
                        mm = three(psum[:, QO, t * D:(t + 1) * D], oT_hi[:, b % 2, p, q], oT_lo[:, b % 2, p, q],
                                   att_hi[:, g % 2, w], att_lo[:, g % 2, w], p == 0, p == 1)
                mm.then_inc(wo_ps, 1)

            proj(0, 0, 0)
            proj(0, 0, 1)
            qkT(0, 0)

            def step(g, b, has1, has2, more):
                nxt, prv = after(g, b), before(g, b)
                scores(g, b, 0)
                if more:
                    proj(*nxt, 0)
                    proj(*nxt, 1)
                if has1:
                    probT(*prv, 1)
                    value(*prv, 0)
                scores(g, b, 1)
                if more:
                    qkT(*nxt)
                if has1:
                    value(*prv, 1)
                probT(g, b, 0)
                if has2:
                    output(*before(*prv), 4 * g + b + 1 + more)

            run_steps(pe, step)
            last = (KV - 1, B - 1)
            probT(*last, 1)
            value(*last, 0)
            value(*last, 1)
            output(*before(*last), 4 * KV)
            output(*last, 4 * KV)

            for n in range(B, 2 * B):
                norm_T(n)
            pe.wait_ge(hl_set, 2 * B)
            pe.wait_ge(pre_pool, 3)
            for tile in range(NT):
                tok = slice(tile * P, (tile + 1) * P)
                for k in range(KD):
                    three(psum[:, 0, tile * E:(tile + 1) * E], actT_hi[:, k, tok], actT_lo[:, k, tok],
                          wg_hi[:, k, :], wg_lo[:, k, :], k == 0, False)
                    mm = pe.matmul(psum[:, 0, tile * E:(tile + 1) * E], actT_lo[:, k, tok], wg_lo[:, k, :],
                                   start=False, stop=k == KD - 1)
            mm.then_inc(logit_ps, 1)
            pe.wait_ge(logit_set, 1)

            def up(e, par, hf, q):
                u = 4 * e + 2 * hf + q
                if hf == 0 and q == 0:
                    pe.wait_ge(expw_split, e + 1)
                wait(pe, prod_set, u - 1)
                tok = slice(hf * 512, (hf + 1) * 512)
                for w, s in ((0, up1_ps), (1, up3_ps)):
                    for k in range(KD):
                        c = slice((w * KD + k) * D + q * P, (w * KD + k) * D + (q + 1) * P)
                        mm = three(psum[:, 2 * q + w, :], exp_hi[:, par, c], exp_lo[:, par, c],
                                   actT_hi[:, k, tok], actT_lo[:, k, tok], k == 0, k == KD - 1)
                    mm.then_inc(s, 1)

            def down(e, par, hf):
                j = 2 * e + hf
                pe.wait_ge(al_set, 2 * j + 2)
                for c in range(2):
                    wait(pe, acc_set, 2 * j - 3 + c)
                    for tt in range(2):
                        tok = slice((2 * c + tt) * P, (2 * c + tt + 1) * P)
                        for q in range(2):
                            w = slice((2 * KD + q) * D, (2 * KD + q + 1) * D)
                            mm = three(psum[:, 4 + 2 * hf + c, tt * D:(tt + 1) * D],
                                       aT_hi[:, hf, q, tok], aT_lo[:, hf, q, tok],
                                       exp_hi[:, par, w], exp_lo[:, par, w], q == 0, q == 1)
                    mm.then_inc(down_ps, 1)

            def halves(ep, first):
                for par in range(2):
                    e = 2 * ep + par
                    for hf in range(2):
                        up(e, par, hf, 0)
                        up(e, par, hf, 1)
                        if hf:
                            down(e, par, 0)
                        elif par:
                            down(e - 1, 0, 1)
                        elif not first:
                            down(e - 1, 1, 1)

            halves(0, True)
            with pe.Fori(1, E // 2) as ep:
                halves(ep, False)
            down(E - 1, 1, 1)

        @block.scalar
        def _(act):
            act.wait_ge(w2_in, 16)
            act.activation(w2_hi[:, :, :], w2_raw[:, :, :], ACT.Copy).then_inc(w2h_set, 1)
            act.wait_ge(small_in, 16)
            act.activation(ident_bf[:, :], ident, ACT.Copy).then_inc(consts_set, 1)
            for b in range(B):
                tok = slice(b * S, (b + 1) * S)
                act.wait_ge(xq_scaled, b + 1)
                for k in range(KD):
                    ins = act.activation(actT_hi[:, k, tok], xa[:, k, tok], ACT.Copy, scale=qemb[:, k, b:b + 1])
                ins.then_inc(xqh_set, 1)

            def squares(n):
                b = n % B
                for t in range(2):
                    ins = act.activation(junk[:, t, :], y[:, 2 * b + t, :], ACT.Square,
                                         accum_out=ss[:, n // B, 2 * b + t:2 * b + t + 1])
                ins.then_inc(sq_set, 1)

            def root(n):
                b = n % B
                c = (slice(None), n // B, slice(2 * b, 2 * b + 2))
                act.wait_ge(var_set, n + 1)
                act.activation(rstd[c], var[c], ACT.Sqrt).then_inc(std_set, 1)

            def norm_hi(n):
                b = n % B
                tok = slice(b * S, (b + 1) * S)
                dst = hT_hi if n < B else actT_hi
                w = SMALL["ln"] if n < B else SMALL["ffln"]
                act.wait_ge(hnT_ps, n + 1)
                for k in range(KD):
                    ins = act.activation(dst[:, k, tok], psum[:, 4 + b, k * S:(k + 1) * S], ACT.Copy,
                                         scale=sm[:, w + k:w + k + 1])
                ins.then_inc(hh_set, 1)

            for n in range(B):
                act.wait_ge(y_set, n + 1)
                squares(n)
                root(n)
            for n in range(B):
                norm_hi(n)

            def exps(g, b, p):
                m = 2 * (4 * g + b) + p
                act.wait_ge(max_set, m + 1)
                wait(act, pT_ps, m - 1)
                for t in range(2):
                    c = slice(t * P, t * P + (t + 1) * P)
                    for h in range(2):
                        ins = act.activation(prob[:, p, h, c], psum[:, S_BANK + h, c], ACT.Exp,
                                             bias=nmax[:, p, t, h:h + 1], accum_out=rsum[:, p, t, h:h + 1])
                ins.then_inc(exp_set, 1)

            def probT_hi(g, b, p):
                m = 2 * (4 * g + b) + p
                act.wait_ge(pT_ps, m + 1)
                wait(act, pv_ps, m - 1)
                act.activation(pT_hi[:, p, :, :], psum[:, PT_BANK:PT_BANK + 2, 0:3 * P], ACT.Copy)\
                   .then_inc(pTh_set, 1)

            def value_hi(g, b, p):
                i = 4 * g + b
                act.wait_ge(pv_ps, 2 * i + p + 1)
                wait(act, wo_ps, i - 1)
                act.activation(oT_hi[:, b % 2, p, :], psum[:, PV, 0:S], ACT.Copy).then_inc(oh_set, 1)

            def qk_hi(g, b):
                i = 4 * g + b
                act.wait_ge(qkT_ps, i + 1)
                act.activation(qT_hi[:, :, :], psum[:, QO, :].rearrange("p (a s) -> p a s", a=2), ACT.Copy)
                act.activation(kT_hi[:, :], psum[:, PJ, 0:S], ACT.Copy).then_inc(qkh_set, 1)

            qk_hi(0, 0)

            def step(g, b, has1, has2, more):
                prv = before(g, b)
                exps(g, b, 0)
                if has1:
                    probT_hi(*prv, 1)
                    value_hi(*prv, 0)
                if more:
                    qk_hi(*after(g, b))
                exps(g, b, 1)
                if has1:
                    value_hi(*prv, 1)
                probT_hi(g, b, 0)

            run_steps(act, step)
            probT_hi(KV - 1, B - 1, 1)
            value_hi(KV - 1, B - 1, 0)
            value_hi(KV - 1, B - 1, 1)

            for n in range(B, 2 * B):
                act.wait_ge(x1_set, 4 * (KV - 1) + n - B + 1)
                squares(n)
                root(n)
            for n in range(B, 2 * B):
                norm_hi(n)
            act.wait_ge(lshift, 1)
            act.activation(expl[:, :, :], expl[:, :, :], ACT.Exp).then_inc(lexp, 1)

            def unit(e, hf, q):
                u = 4 * e + 2 * hf + q
                j = 2 * e + hf
                act.wait_ge(up1_ps, u + 1)
                wait(act, prod_set, u - 1)
                act.activation(sil[:, q, :], psum[:, 2 * q, :], ACT.Silu).then_inc(sil_set, 1)
                act.wait_ge(prod_set, u + 1)
                wait(act, down_ps, 2 * j - 2)
                act.activation(aT_hi[:, hf, q, :], prod[:, q, :], ACT.Copy).then_inc(ah_set, 1)

            for hf in range(2):
                for q in range(2):
                    unit(0, hf, q)
            with act.Fori(1, E) as e:
                for hf in range(2):
                    for q in range(2):
                        unit(e, hf, q)

        @block.vector
        def _(dve):
            count = [0]

            def chain(ins):
                count[0] += 1
                ins.then_inc(pre_dve, 1)
                dve.wait_ge(pre_dve, count[0])

            dve.memset(ones[:, :], 1.0).then_inc(zeros_set, 1)
            dve.memset(v_hi[:, :, :, :].bitcast(F32), 0.0).then_inc(zeros_set, 1)
            dve.memset(v_lo[:, :, :, :].bitcast(F32), 0.0).then_inc(zeros_set, 1)
            dve.wait_ge(qemb_ps, 1)
            for k in range(KD):
                chain(dve.tensor_scalar(qemb[:, k, :], psum[:, 4, k * B:(k + 1) * B],
                                        sm[:, SMALL["b3"] + k:SMALL["b3"] + k + 1], 0.0, ALU.add, ALU.max))
            for b in range(B):
                tok = slice(b * S, (b + 1) * S)
                dve.wait_ge(x_in[b], 16)
                chain(dve.tensor_reduce(vsum[:, b, :], xTs[:, :, tok], X, ALU.add))
                for k in range(KD):
                    ins = dve.tensor_scalar(xa[:, k, tok], xTs[:, k, tok], float(S), vsum[:, b, k:k + 1],
                                            ALU.mult, ALU.add)
                ins.then_inc(xq_scaled, 1)
                dve.wait_ge(xqh_set, b + 1)
                for k in range(KD):
                    ins = dve.scalar_tensor_tensor(out=actT_lo[:, k, tok], in0=xa[:, k, tok],
                                                   scalar=qemb[:, k, b:b + 1],
                                                   in1=actT_hi[:, k, tok].bitcast(F32),
                                                   op0=ALU.mult, op1=ALU.subtract)
                ins.then_inc(xql_set, 1)
            for b in range(B):
                dve.wait_ge(cond_ps, b + 1)
                dve.tensor_scalar(y[:, 2 * b:2 * b + 2, :],
                                  psum[:, b, :].rearrange("p (t d) -> p t d", t=2), 0.0, None, ALU.max)\
                   .then_inc(y_set, 1)

            def variance(n):
                b = n % B
                c = (slice(None), n // B, slice(2 * b, 2 * b + 2))
                dve.wait_ge(sq_set, n + 1)
                dve.tensor_scalar(var[c], ss[c], 1.0 / D, EPS, ALU.mult, ALU.add).then_inc(var_set, 1)

            def normed(n):
                b = n % B
                c = (slice(None), n // B, slice(2 * b, 2 * b + 2))
                dve.wait_ge(std_set, n + 1)
                chain(dve.reciprocal(rstd[c], rstd[c]))
                chain(dve.tensor_tensor(nt1[c], rstd[c], rstd[c], ALU.mult))
                chain(dve.tensor_tensor(nt1[c], nt1[c], var[c], ALU.mult))
                chain(dve.tensor_scalar(nt1[c], nt1[c], -0.5, 1.5, ALU.mult, ALU.add))
                chain(dve.tensor_tensor(rstd[c], rstd[c], nt1[c], ALU.mult))
                wait(dve, hnT_ps, n - 1)
                for t in range(2):
                    ins = dve.tensor_scalar(hn[:, n % 2, t, :], y[:, 2 * b + t, :],
                                            rstd[:, n // B, 2 * b + t:2 * b + t + 1], None, ALU.mult)
                ins.then_inc(hn_set, 1)

            def norm_lo(n):
                b = n % B
                tok = slice(b * S, (b + 1) * S)
                hi, lo = (hT_hi, hT_lo) if n < B else (actT_hi, actT_lo)
                w = SMALL["ln"] if n < B else SMALL["ffln"]
                dve.wait_ge(hh_set, n + 1)
                for k in range(KD):
                    ins = dve.scalar_tensor_tensor(out=lo[:, k, tok], in0=psum[:, 4 + b, k * S:(k + 1) * S],
                                                   scalar=sm[:, w + k:w + k + 1],
                                                   in1=hi[:, k, tok].bitcast(F32),
                                                   op0=ALU.mult, op1=ALU.subtract)
                ins.then_inc(hl_set, 1)

            for n in range(B):
                variance(n)
                normed(n)
            for n in range(B):
                norm_lo(n)

            def columns(g, b, t):
                i = 4 * g + b
                dve.wait_ge(proj_ps, 2 * i + t + 1)
                if isinstance(g, int) and g == 0 and b == 0 and t == 0:
                    dve.wait_ge(rope_in, 16)
                    dve.wait_ge(zeros_set, 3)
                wait(dve, rope_add, i)
                dve.tensor_tensor(rc[:, t, :], psum[:, PJ + t, 0:ROT], rope_sb[:, 0, t, :], ALU.mult)
                dve.tensor_tensor(rs_[:, t, :], psum[:, PJ + t, 0:ROT], rope_sb[:, 1, t, :], ALU.mult)\
                   .then_inc(rope_mul, 1)
                mid = slice(HD, 2 * HD)
                dve.tensor_copy(v_hi[:, b, t, mid], psum[:, PJ + t, ROT:QKV]).then_inc(vh_set, 1)
                dve.wait_ge(vh_set, 2 * i + t + 1)
                dve.tensor_tensor(v_lo[:, b, t, mid], psum[:, PJ + t, ROT:QKV],
                                  v_hi[:, b, t, mid].bitcast(F32), ALU.subtract).then_inc(vl_set, 1)

            def qk_lo(g, b):
                dve.wait_ge(qkh_set, 4 * g + b + 1)
                dve.tensor_tensor(qT_lo[:, :, :], psum[:, QO, :].rearrange("p (a s) -> p a s", a=2),
                                  qT_hi[:, :, :].bitcast(F32), ALU.subtract)
                dve.tensor_tensor(kT_lo[:, :], psum[:, PJ, 0:S], kT_hi[:, :].bitcast(F32), ALU.subtract)\
                   .then_inc(qkl_set, 1)

            def maxima(g, b, p):
                m = 2 * (4 * g + b) + p
                dve.wait_ge(score_ps, m + 1)
                for t in range(2):
                    ins = dve.tensor_reduce(nmax[:, p, t, :],
                                            psum[:, S_BANK:S_BANK + 2, t * P:t * P + (t + 1) * P],
                                            X, ALU.max, negate=True)
                ins.then_inc(max_set, 1)

            def inverse(g, b, p):
                dve.wait_ge(exp_set, 2 * (4 * g + b) + p + 1)
                dve.reciprocal(rinv[:, p, :, :], rsum[:, p, :, :]).then_inc(inv_set, 1)

            def probT_lo(g, b, p):
                dve.wait_ge(pTh_set, 2 * (4 * g + b) + p + 1)
                dve.tensor_tensor(pT_lo[:, p, :, :], psum[:, PT_BANK:PT_BANK + 2, 0:3 * P],
                                  pT_hi[:, p, :, :].bitcast(F32), ALU.subtract).then_inc(pTl_set, 1)

            def value_lo(g, b, p):
                dve.wait_ge(oh_set, 2 * (4 * g + b) + p + 1)
                dve.tensor_tensor(oT_lo[:, b % 2, p, :], psum[:, PV, 0:S], oT_hi[:, b % 2, p, :].bitcast(F32),
                                  ALU.subtract).then_inc(ol_set, 1)

            def residual(g, b):
                dve.wait_ge(wo_ps, 4 * g + b + 1)
                yb = y[:, 2 * b:2 * b + 2, :]
                dve.tensor_tensor(yb, psum[:, QO, :].rearrange("p (t d) -> p t d", t=2), yb, ALU.add)\
                   .then_inc(x1_set, 1)

            columns(0, 0, 0)
            columns(0, 0, 1)
            qk_lo(0, 0)

            def step(g, b, has1, has2, more):
                nxt, prv = after(g, b), before(g, b)
                maxima(g, b, 0)
                if more:
                    columns(*nxt, 0)
                    columns(*nxt, 1)
                inverse(g, b, 0)
                if has1:
                    probT_lo(*prv, 1)
                    value_lo(*prv, 0)
                maxima(g, b, 1)
                if more:
                    qk_lo(*nxt)
                inverse(g, b, 1)
                if has1:
                    value_lo(*prv, 1)
                probT_lo(g, b, 0)
                if has2:
                    residual(*before(*prv))

            run_steps(dve, step)
            probT_lo(KV - 1, B - 1, 1)
            value_lo(KV - 1, B - 1, 0)
            value_lo(KV - 1, B - 1, 1)
            residual(KV - 1, B - 2)
            residual(KV - 1, B - 1)

            for n in range(B, 2 * B):
                variance(n)
                normed(n)
            for n in range(B, 2 * B):
                norm_lo(n)
            dve.wait_ge(logit_ps, 1)
            dve.memset(logit[:, :, E:E + 4], BIG)
            lg = psum[:, 0, 0:NT * E].rearrange("p (t e) -> p t e", t=NT)
            dve.tensor_copy(logit[:, :, 0:E], lg).then_inc(logit_set, 1)
            dve.wait_ge(logit_set, 1)
            for tile in range(NT):
                ins = dve.max(top[:, tile, :], logit[:, tile, 0:E])
            chain(ins)
            chain(dve.tensor_tensor(expl[:, :, :], logit[:, :, 0:E], top[:, :, 0:1].to_broadcast([P, NT, E]),
                                    ALU.subtract))
            dve.memset(top[:, :, TOPK:8], BIG).then_inc(lshift, 1)
            dve.wait_ge(lshift, 1)
            for tile in range(NT):
                ins = dve.match_replace(left[:, tile, :], top[:, tile, :], logit[:, tile, :], -BIG)
            chain(ins)
            chain(dve.tensor_tensor(chosen[:, :, :], left[:, :, 0:E], logit[:, :, 0:E], ALU.not_equal))
            dve.wait_ge(lexp, 1)
            chain(dve.tensor_tensor(chosen[:, :, :], chosen[:, :, :], expl[:, :, :], ALU.mult))
            chain(dve.tensor_reduce(gsum[:, :], chosen[:, :, :], X, ALU.add))
            chain(dve.reciprocal(gsum[:, :], gsum[:, :]))
            chain(dve.tensor_tensor(gates[:, :, :], chosen[:, :, :], gsum[:, :, None].to_broadcast([P, NT, E]),
                                    ALU.mult))
            dve.wait_ge(xn_in, 16)
            chain(dve.tensor_tensor(y[:, :, :], y[:, :, :], x_sb[:, :, :], ALU.add))

            def product(e, hf, q):
                u = 4 * e + 2 * hf + q
                dve.wait_ge(sil_set, u + 1)
                dve.wait_ge(up3_ps, u + 1)
                wait(dve, ah_set, u - 1)
                dve.tensor_tensor(prod[:, q, :], psum[:, 2 * q + 1, :], sil[:, q, :], ALU.mult)\
                   .then_inc(prod_set, 1)
                dve.wait_ge(ah_set, u + 1)
                dve.tensor_tensor(aT_lo[:, hf, q, :], prod[:, q, :], aT_hi[:, hf, q, :].bitcast(F32),
                                  ALU.subtract).then_inc(al_set, 1)

            def accumulate(e, hf):
                j = 2 * e + hf
                for c in range(2):
                    dve.wait_ge(down_ps, 2 * j + c + 1)
                    for tt in range(2):
                        tile = 4 * hf + 2 * c + tt
                        ins = dve.scalar_tensor_tensor(out=y[:, tile, :],
                                                       in0=psum[:, 4 + 2 * hf + c, tt * D:(tt + 1) * D],
                                                       scalar=gates[:, tile, bass.ds(e, 1)], in1=y[:, tile, :],
                                                       op0=ALU.mult, op1=ALU.add)
                    ins.then_inc(acc_set, 1)

            def expert(e, first):
                for hf in range(2):
                    product(e, hf, 0)
                    product(e, hf, 1)
                    if hf:
                        accumulate(e, 0)
                    elif not first:
                        accumulate(e - 1, 1)

            expert(0, True)
            with dve.Fori(1, E) as e:
                expert(e, False)
            accumulate(E - 1, 1)

        @block.gpsimd
        def _(pool):
            n_self = [0]

            def chain(ins):
                n_self[0] += 1
                ins.then_inc(pre_pool, 1)
                pool.wait_ge(pre_pool, n_self[0])

            def times_one(dst, src, shape):
                return pool.tensor_tensor(dst, src, ones[:, 0:1].to_broadcast(shape), ALU.mult)

            pool.wait_ge(w2h_set, 1)
            pool.tensor_tensor(w2_lo[:, :, :], w2_raw[:, :, :], w2_hi[:, :, :].bitcast(F32), ALU.subtract)\
                .then_inc(w2_split, 1)

            def split(hi, lo, raw, n, hi_set, count):
                times_one(hi, raw, [P, n]).then_inc(hi_set, 1)
                pool.wait_ge(hi_set, count)
                return pool.tensor_tensor(lo, raw, hi.bitcast(F32), ALU.subtract)

            def split_proj(g):
                pool.wait_ge(attw_in, 16 * (g + 1))
                if not isinstance(g, int) or g > 1:
                    pool.wait_ge(proj_ps, 8 * (g - 1))
                split(att_hi[:, g % 2, 0:WQ], att_lo[:, g % 2, 0:WQ], att_raw[:, 0:WQ], WQ, atth_set, 2 * g + 1)\
                    .then_inc(attw_split, 1)

            def split_out(g):
                if not isinstance(g, int) or g > 1:
                    pool.wait_ge(wo_ps, 4 * (g - 1))
                split(att_hi[:, g % 2, WQ:], att_lo[:, g % 2, WQ:], att_raw[:, WQ:], WO, atth_set, 2 * g + 2)\
                    .then_inc(attwo_split, 1)

            pool.wait_ge(zeros_set, 1)
            split_proj(0)
            split_out(0)
            wg = sm[:, SMALL["wg"]:SMALL["wg"] + KD * E].rearrange("p (k e) -> p k e", k=KD)
            pool.wait_ge(small_in, 16)
            chain(times_one(wg_hi[:, 0, :], wg[:, 0, :], [P, E]))
            chain(times_one(wg_hi[:, 1, :], wg[:, 1, :], [P, E]))
            chain(pool.tensor_tensor(wg_lo[:, :, :], wg, wg_hi[:, :, :].bitcast(F32), ALU.subtract))

            def rope(g, b):
                i = 4 * g + b
                pool.wait_ge(rope_mul, 2 * i + 2)
                wait(pool, qkT_ps, i)
                c = rc[:, :, :].rearrange("p t (h a e) -> p t h a e", a=2, e=HD // 2)
                s = rs_[:, :, :].rearrange("p t (h a e) -> p t h a e", a=2, e=HD // 2)
                r = rot[:, :, :].rearrange("p t (h a e) -> p t h a e", a=2, e=HD // 2)
                for a in range(2):
                    pool.tensor_tensor(r[:, :, 0:GH + 1, a, :], c[:, :, :, a, :], s[:, :, :, 1 - a, :], ALU.add)
                for a in range(2):
                    ins = pool.tensor_tensor(r[:, :, GH + 1, a, :], c[:, :, GH, a, :], s[:, :, GH, 1 - a, :],
                                             ALU.add)
                ins.then_inc(rope_add, 1)

            def normalise(g, b, p):
                pool.wait_ge(inv_set, 2 * (4 * g + b) + p + 1)
                for t in range(2):
                    w = (t + 1) * P
                    pr = prob[:, p, :, t * P:t * P + w]
                    ins = pool.tensor_tensor(pr, pr, rinv[:, p, t, :, None].to_broadcast([P, 2, w]), ALU.mult)
                ins.then_inc(norm_set, 1)

            rope(0, 0)

            def step(g, b, has1, has2, more):
                if more:
                    rope(*after(g, b))
                normalise(g, b, 0)
                normalise(g, b, 1)
                if not (isinstance(g, int) and g == KV - 1):
                    if b == 1:
                        split_proj(g + 1)
                    elif b == 2:
                        split_out(g + 1)

            run_steps(pool, step)

            def split_exp(e, par):
                pool.wait_ge(expw_in[par], 16 * (e // 2 + 1) if isinstance(e, int) else 8 * (e - par) + 16)
                wait(pool, down_ps, 4 * (e - 1))
                times_one(exp_hi[:, par, :], exp_raw[:, par, :], [P, EW]).then_inc(exph_set, 1)
                pool.wait_ge(exph_set, e + 1)
                pool.tensor_tensor(exp_lo[:, par, :], exp_raw[:, par, :], exp_hi[:, par, :].bitcast(F32),
                                   ALU.subtract).then_inc(expw_split, 1)

            pool.wait_ge(wo_ps, 4 * KV)
            pool.wait_ge(x1_set, 4 * KV)
            split_exp(0, 0)
            split_exp(1, 1)
            with pool.Fori(1, E // 2) as ep:
                for par in range(2):
                    split_exp(2 * ep + par, par)


def kernel(x, cond_1024, L0_cond_W3, L0_cond_b3, L0_cond_W2, L0_cond_b2, L0_ffn_ln_w, L0_ffn_ff_ln_w,
           L0_ffn_wq, L0_ffn_wk, L0_ffn_wv, L0_ffn_wo, L0_ffn_wg, L0_ffn_w1, L0_ffn_w3, L0_ffn_w2):
    import ml_dtypes
    import concourse.bacc as _bacc
    from concourse.bass_utils import run_bass_kernel_spmd as _run

    def a(v):
        return np.asarray(v)

    def cols(v):
        return a(v).reshape(KD, P).T

    def rows(w):
        w = a(w)
        return w.reshape(-1, P, w.shape[-1]).transpose(1, 0, 2)

    xf = a(x).reshape(B * S, D)
    small = np.concatenate([a(cond_1024).T, cols(L0_cond_b3), cols(L0_ffn_ln_w), cols(L0_ffn_ff_ln_w),
                            rows(L0_ffn_wg).reshape(P, KD * E), np.eye(P, dtype=np.float32)], axis=1)
    wq = rows(L0_ffn_wq).reshape(P, KD, KV, GH * HD)
    wk = rows(L0_ffn_wk).reshape(P, KD, KV, HD)
    wv = rows(L0_ffn_wv).reshape(P, KD, KV, HD)
    qkv = np.concatenate([wq, wk, wv], axis=3).transpose(2, 0, 1, 3).reshape(KV, P, WQ)
    wo = a(L0_ffn_wo).reshape(KV, 2, P, D).transpose(0, 2, 1, 3).reshape(KV, P, WO)
    attw = np.concatenate([qkv, wo], axis=2)
    expw = np.stack([a(w).reshape(E, KD, P, D).transpose(0, 2, 1, 3) for w in (L0_ffn_w1, L0_ffn_w3, L0_ffn_w2)],
                    axis=2).reshape(E, P, EW)
    half = HD // 2
    inv = (np.float32(1.0) / np.float32(150000.0) ** (np.arange(half, dtype=np.float32) / np.float32(half)))
    ang = np.arange(S, dtype=np.float32)[:, None] * inv.astype(np.float32)
    cos, sin = np.cos(ang), np.sin(ang)
    scale = np.array([HD ** -0.5] * GH + [1.0], np.float32)[None, :, None, None]
    tab = np.stack([np.stack([cos, cos], 1)[:, None] * scale, np.stack([sin, -sin], 1)[:, None] * scale])
    rope = tab.astype(np.float32).reshape(2, 2, P, ROT).transpose(2, 0, 1, 3)
    mask = np.triu(np.full((P, P), -1e30, np.float32), 1).astype(ml_dtypes.bfloat16)

    data = dict(small=small, w3=a(L0_cond_W3), w2c=a(L0_cond_W2), b2=a(L0_cond_b2).reshape(1, D), xT=xf.T,
                xn=xf, rope=rope, mask=mask, attw=attw, expw=expw)
    nc = _bacc.Bacc("TRN2", target_bir_lowering=False, num_devices=1)
    arrays, args = {}, {}
    for name, v in data.items():
        v = np.ascontiguousarray(v)
        arrays["in_" + name] = v
        args[name] = nc.dram_tensor("in_" + name, v.shape, mybir.dt.from_np(v.dtype), kind="ExternalInput").ap()
    res = nc.dram_tensor("res", (B * S, D), F32, kind="ExternalOutput").ap()
    build(nc, out=res, **args)
    r = _run(nc, [arrays], core_ids=[0])
    return r.results[0]["res"].reshape(B, S, D)
```

```python
from contextlib import ExitStack

import numpy as np
import concourse.bass as bass
from concourse import mybir
from concourse.alu_op_type import AluOpType as ALU

F32 = mybir.dt.float32
F32R = mybir.dt.float32r
BF16 = mybir.dt.bfloat16
ACT = mybir.ActivationFunctionType
X = mybir.AxisListType.X

P = 128
B, S, D = 4, 256, 256
NT = B * S // P
KD = D // P
HEADS, KV, HD = 32, 8, 64
GH = HEADS // KV
E, TOPK = 16, 4
EPS = 1e-5
QKV = GH * HD + 2 * HD
ROT = (GH + 1) * HD
WQ, WO = KD * QKV, 2 * D
EW = 3 * KD * D
BIG = 3.0e38
SMALL = dict(cond=0, b3=4, ln=6, ffln=8, wg=10, ident=42)
NSMALL = 170


def build(nc, small, w3, w2c, b2, xT, xn, rope, mask, attw, expw, out):
    with ExitStack() as outer:
        def sem(name):
            return outer.enter_context(nc.semaphore(name))

        def keep(name, shape, dt=F32):
            return outer.enter_context(nc.sbuf_tensor(name, shape, dt))

        sm = keep("sm", [P, NSMALL])
        ident = sm[:, SMALL["ident"]:SMALL["ident"] + P]
        ident_bf = keep("ident_bf", [P, P], BF16)
        mask_sb = keep("mask_sb", [P, P], BF16)
        ones = keep("ones", [P, P])
        y = keep("y", [P, NT, D])
        actT_hi = keep("actT_hi", [P, KD, B * S], F32R)
        actT_lo = keep("actT_lo", [P, KD, B * S], F32R)
        ss = keep("ss", [P, 2, NT])
        var = keep("var", [P, 2, NT])
        rstd = keep("rstd", [P, 2, NT])
        nt1 = keep("nt1", [P, 2, NT])
        hn = keep("hn", [P, 2, 2, D])
        junk = keep("junk", [P, 2, D])
        exp_raw = keep("exp_raw", [P, 2, EW])
        wg2 = keep("wg2", [P, KD, 2, E], F32R)
        eps = keep("eps", [P, 1])
        root_eps = keep("root_eps", [P, 1])
        gates = keep("gates", [P, NT, E])
        psum = outer.enter_context(nc.psum_tensor("psum", [P, 8, 512], F32))

        def tmp(name, shape, dt=F32):
            return keep(name, shape, dt)

        att_raw = tmp("att_raw", [P, WQ + WO])
        att_hi = tmp("att_hi", [P, 2, WQ + WO], F32R)
        att_lo = tmp("att_lo", [P, 2, WQ + WO], F32R)
        rope_sb = tmp("rope_sb", [P, 2, 2, ROT])
        rc = tmp("rc", [P, 2, ROT])
        rs_ = tmp("rs_", [P, 2, ROT])
        rot = tmp("rot", [P, 2, ROT + HD])
        qT_hi = tmp("qT_hi", [P, 2, S], F32R)
        qT_lo = tmp("qT_lo", [P, 2, S], F32R)
        kT_hi = tmp("kT_hi", [P, S], F32R)
        kT_lo = tmp("kT_lo", [P, S], F32R)
        v_hi = tmp("v_hi", [P, B, 2, 2, HD], F32R)
        v_lo = tmp("v_lo", [P, B, 2, 2, HD], F32R)
        prob = tmp("prob", [P, 2, 2, 3 * P])
        pT_hi = tmp("pT_hi", [P, 2, 2, 3 * P], F32R)
        pT_lo = tmp("pT_lo", [P, 2, 2, 3 * P], F32R)
        nmax = tmp("nmax", [P, 2, 2, 2])
        rsum = tmp("rsum", [P, 2, 2, 2])
        rinv = tmp("rinv", [P, 2, 2, 2])
        oT_hi = tmp("oT_hi", [P, 2, 2, S], F32R)
        oT_lo = tmp("oT_lo", [P, 2, 2, S], F32R)
        exp_hi = tmp("exp_hi", [P, 2, EW], F32R)
        exp_lo = tmp("exp_lo", [P, 2, EW], F32R)
        logT = tmp("logT", [2 * E, B * S])
        logit = tmp("logit", [P, NT, E + 4])
        top = tmp("top", [P, NT, 8])
        left = tmp("left", [P, NT, E + 4])
        chosen = tmp("chosen", [P, NT, E])
        expl = tmp("expl", [P, NT, E])
        gsum = tmp("gsum", [P, NT])

        with ExitStack() as early:
            def etmp(name, shape, dt=F32):
                return early.enter_context(nc.sbuf_tensor(name, shape, dt))

            hT_hi = etmp("hT_hi", [P, KD, B * S], F32R)
            hT_lo = etmp("hT_lo", [P, KD, B * S], F32R)
            xTs = etmp("xTs", [P, KD, B * S])
            xa = etmp("xa", [P, KD, B * S])
            w3_sb = etmp("w3_sb", [P, D])
            w2_raw = etmp("w2_raw", [P, KD, D])
            w2_hi = etmp("w2_hi", [P, KD, D], F32R)
            w2_lo = etmp("w2_lo", [P, KD, D], F32R)
            b2_sb = etmp("b2_sb", [1, 2 * D])
            b2_parts = etmp("b2_parts", [1, 2, 2 * D], F32R)
            ones_r = etmp("ones_r", [1, P], F32R)
            vsum = etmp("vsum", [P, B, KD])
            vq = etmp("vq", [P, B, KD])
            qemb = etmp("qemb", [P, KD, B])
            qs = etmp("qs", [P, KD, B])

        with ExitStack() as late:
            def etmp(name, shape, dt=F32):
                return late.enter_context(nc.sbuf_tensor(name, shape, dt))

            x_sb = etmp("x_sb", [P, NT, D])
            sil = etmp("sil", [P, 2, 512])
            prod = etmp("prod", [P, 2, 512])
            aT_hi = etmp("aT_hi", [P, 2, 2, 512], F32R)
            aT_lo = etmp("aT_lo", [P, 2, 2, 512], F32R)

        small_in = sem("small_in")
        cond_in = sem("cond_in")
        w2_in = sem("w2_in")
        x_in = [sem(f"x_in{b}") for b in range(B)]
        rope_in = sem("rope_in")
        mask_in = sem("mask_in")
        attw_in = sem("attw_in")
        expw_in = [sem("expw_in0"), sem("expw_in1")]
        xn_in = sem("xn_in")
        stored = sem("stored")
        consts_set = sem("consts_set")
        ones_set = sem("ones_set")
        qemb_ps = sem("qemb_ps")
        pre_dve = sem("pre_dve")
        w2h_set = sem("w2h_set")
        w2_split = sem("w2_split")
        pre_pool = sem("pre_pool")
        xsum_set = sem("xsum_set")
        vq_set = sem("vq_set")
        xqh_set = sem("xqh_set")
        xql_set = sem("xql_set")
        cond_ps = sem("cond_ps")
        y_set = sem("y_set")
        sq_set = sem("sq_set")
        std_set = sem("std_set")
        hn_set = sem("hn_set")
        hnT_ps = sem("hnT_ps")
        hh_set = sem("hh_set")
        hl_set = sem("hl_set")
        attw_split = sem("attw_split")
        attwo_split = sem("attwo_split")
        atth_set = sem("atth_set")
        proj_ps = sem("proj_ps")
        rope_mul = sem("rope_mul")
        vh_set = sem("vh_set")
        vl_set = sem("vl_set")
        rope_add = sem("rope_add")
        qkT_ps = sem("qkT_ps")
        qkh_set = sem("qkh_set")
        qkl_set = sem("qkl_set")
        score_ps = sem("score_ps")
        max_set = sem("max_set")
        exp_set = sem("exp_set")
        inv_set = sem("inv_set")
        norm_set = sem("norm_set")
        pT_ps = sem("pT_ps")
        pTh_set = sem("pTh_set")
        pTl_set = sem("pTl_set")
        pv_ps = sem("pv_ps")
        oh_set = sem("oh_set")
        ol_set = sem("ol_set")
        wo_ps = sem("wo_ps")
        x1_set = sem("x1_set")
        logit_ps = sem("logit_ps")
        logT_set = sem("logT_set")
        logitT_ps = sem("logitT_ps")
        xadd_set = sem("xadd_set")
        logit_set = sem("logit_set")
        lshift = sem("lshift")
        lexp = sem("lexp")
        expw_split = sem("expw_split")
        exph_set = sem("exph_set")
        up1_ps = sem("up1_ps")
        up3_ps = sem("up3_ps")
        sil_set = sem("sil_set")
        prod_set = sem("prod_set")
        ah_set = sem("ah_set")
        al_set = sem("al_set")
        down_ps = sem("down_ps")
        acc_set = sem("acc_set")

        block = outer.enter_context(nc.Block())

        PJ, QT, PV = 4, 6, 7
        S_BANK, PT_BANK = 0, 2
        NORM_BANK = (7, 3, 7, 3, 4, 6, 4, 6)
        LOGT_BANK, LOGIT_BANK = (7, 5), 4
        LAST = 4 * KV - 1

        def before(g, b):
            return (g, b - 1) if b else (g - 1, B - 1)

        def after(g, b):
            return (g, b + 1) if b < B - 1 else (g + 1, 0)

        def run_steps(eng, step):
            for b in range(B):
                step(0, b, b >= 1, b >= 2, True)
            with eng.Fori(1, KV - 1) as g:
                for b in range(B):
                    step(g, b, True, True, True)
            for b in range(B):
                step(KV - 1, b, True, True, b < B - 1)

        def wait(eng, s, count):
            if not isinstance(count, int) or count > 0:
                eng.wait_ge(s, count)

        @block.sync
        def _(sp):
            sp.dma_start(sm[:, :], small).then_inc(small_in, 16)
            sp.dma_start(w3_sb[:, :], w3).then_inc(cond_in, 16)
            xv = xT.rearrange("(k p) (b s) -> b p k s", p=P, b=B)
            for b in range(B):
                sp.dma_start(xTs[:, :, b * S:(b + 1) * S], xv[b]).then_inc(x_in[b], 16)
                if b == 0:
                    sp.dma_start(w2_raw[:, :, :], w2c.rearrange("(k p) n -> p k n", p=P)).then_inc(w2_in, 16)
                    sp.dma_start(b2_sb[:, 0:D], b2).then_inc(cond_in, 16)
                    sp.dma_start(b2_sb[:, D:], b2).then_inc(cond_in, 16)
            sp.dma_start(att_raw[:, :], attw[0]).then_inc(attw_in, 16)
            sp.dma_start(rope_sb[:, :, :, :], rope).then_inc(rope_in, 16)
            sp.dma_start(mask_sb[:, :], mask).then_inc(mask_in, 16)
            for e in range(2):
                sp.dma_start(exp_raw[:, e, :], expw[e]).then_inc(expw_in[e], 16)
            with sp.Fori(1, KV) as g:
                sp.wait_ge(attwo_split, g)
                sp.dma_start(att_raw[:, :], attw[g]).then_inc(attw_in, 16)
            sp.wait_ge(proj_ps, 8 * KV)
            sp.dma_start(x_sb[:, :, :], xn.rearrange("(t p) d -> p t d", p=P)).then_inc(xn_in, 16)
            with sp.Fori(1, E // 2) as ep:
                for par in range(2):
                    sp.wait_ge(expw_split, 2 * ep + par - 1)
                    sp.dma_start(exp_raw[:, par, :], expw[2 * ep + par]).then_inc(expw_in[par], 16)
            ov = out.rearrange("(t p) d -> p t d", p=P)
            for c in range(4):
                sp.wait_ge(acc_set, 4 * (E - 1) + c + 1)
                sp.dma_start(ov[:, 2 * c:2 * c + 2, :], y[:, 2 * c:2 * c + 2, :]).then_inc(stored, 16)
            sp.wait_ge(stored, 64)

        @block.tensor
        def _(pe):
            def three(out_ap, sh, sl, mh, ml, start, stop):
                pe.matmul(out_ap, sh, mh, start=start, stop=False)
                pe.matmul(out_ap, sh, ml, start=False, stop=False)
                return pe.matmul(out_ap, sl, mh, start=False, stop=stop)

            pe.wait_ge(small_in, 16)
            pe.wait_ge(cond_in, 48)
            for k in range(KD):
                mm = pe.matmul(psum[:, 4, k * B:(k + 1) * B], w3_sb[:, k * P:(k + 1) * P],
                               sm[:, 0:B], start=True, stop=True)
            mm.then_inc(qemb_ps, 1)
            pe.wait_ge(w2_split, 1)
            for b in range(B):
                for part in range(2):
                    pe.matmul(psum[:, b, :], ones_r[0:1, :], b2_parts[:, part, :], start=part == 0, stop=False)
            pe.wait_ge(w2_split, 2)
            for b in range(B):
                pe.wait_ge(xql_set, b + 1)
                for t in range(2):
                    tok = slice(b * S + t * P, b * S + (t + 1) * P)
                    for k in range(KD):
                        mm = three(psum[:, b, t * D:(t + 1) * D], actT_hi[:, k, tok], actT_lo[:, k, tok],
                                   w2_hi[:, k, :], w2_lo[:, k, :], False, t == 1 and k == KD - 1)
                mm.then_inc(cond_ps, 1)

            def norm_T(n):
                pe.wait_ge(hn_set, n + 1)
                if n % B >= 2:
                    pe.wait_ge(hl_set, n - 1)
                elif n == 1:
                    pe.wait_ge(y_set, B)
                for k in range(KD):
                    for t in range(2):
                        mm = pe.transpose(psum[:, NORM_BANK[n], k * S + t * P:k * S + (t + 1) * P],
                                          hn[:, n % 2, t, k * P:(k + 1) * P], ident)
                mm.then_inc(hnT_ps, 1)

            def proj(g, b, t):
                i = 4 * g + b
                if t == 0:
                    pe.wait_ge(attw_split, g + 1)
                    wait(pe, qkl_set, i)
                else:
                    wait(pe, x1_set, i - 3)
                if isinstance(g, int) and g == 0:
                    pe.wait_ge(hl_set, b + 1)
                tok = slice(b * S + t * P, b * S + (t + 1) * P)
                for k in range(KD):
                    w = slice(k * QKV, (k + 1) * QKV)
                    mm = three(psum[:, PJ + t, 0:QKV], hT_hi[:, k, tok], hT_lo[:, k, tok],
                               att_hi[:, g % 2, w], att_lo[:, g % 2, w], k == 0, k == KD - 1)
                mm.then_inc(proj_ps, 1)

            def qkT(g, b):
                i = 4 * g + b
                pe.wait_ge(rope_add, i + 1)
                pe.wait_ge(vl_set, 2 * i + 2)
                for p in range(2):
                    for t in range(2):
                        pe.transpose(psum[:, QT, p * S + t * P:p * S + (t + 1) * P],
                                     rot[:, t, p * P:(p + 1) * P], ident)
                for t in range(2):
                    mm = pe.transpose(psum[:, PJ, t * P:(t + 1) * P], rot[:, t, 2 * P:3 * P], ident)
                mm.then_inc(qkT_ps, 1)

            def scores(g, b, p):
                i = 4 * g + b
                m = 2 * i + p
                pe.wait_ge(qkl_set, i + 1)
                wait(pe, exp_set, m)
                if isinstance(g, int) and g == 0 and b == 0 and p == 0:
                    pe.wait_ge(mask_in, 16)
                    pe.wait_ge(consts_set, 1)
                for t in range(2):
                    keys, cols = slice(0, (t + 1) * P), slice(t * P, t * P + (t + 1) * P)
                    q = slice(t * P, (t + 1) * P)
                    for n, (qs, ks) in enumerate(((qT_hi, kT_hi), (qT_hi, kT_lo), (qT_lo, kT_hi))):
                        for h in range(2):
                            r = slice(h * HD, (h + 1) * HD)
                            pe.matmul(psum[:, S_BANK + h, cols], qs[r, p, q], ks[r, keys],
                                      start=n == 0, stop=False)
                    for h in range(2):
                        mm = pe.matmul(psum[:, S_BANK + h, 2 * t * P:(2 * t + 1) * P], ident_bf[:, :],
                                       mask_sb[:, :], start=False, stop=True)
                mm.then_inc(score_ps, 1)

            def probT(g, b, p):
                m = 2 * (4 * g + b) + p
                pe.wait_ge(norm_set, m + 1)
                wait(pe, pTl_set, m)
                if isinstance(g, int) and m == 0:
                    pe.wait_ge(hl_set, B)
                for h in range(2):
                    for blk in range(3):
                        mm = pe.transpose(psum[:, PT_BANK + h, blk * P:(blk + 1) * P],
                                          prob[:, p, h, blk * P:(blk + 1) * P], ident)
                mm.then_inc(pT_ps, 1)

            def value(g, b, p):
                m = 2 * (4 * g + b) + p
                pe.wait_ge(pTl_set, m + 1)
                wait(pe, ol_set, m)
                pv = psum[:, PV, :].rearrange("p (h s) -> p h s", h=2)
                for kt in range(2):
                    pt = slice(2 * kt * P, 2 * kt * P + S - kt * P)
                    mm = three(pv[:, :, kt * P:S],
                               v_hi[:, b, kt, :, :].rearrange("p a e -> p (a e)"),
                               v_lo[:, b, kt, :, :].rearrange("p a e -> p (a e)"),
                               pT_hi[:, p, :, pt], pT_lo[:, p, :, pt], kt == 0, kt == 1)
                mm.then_inc(pv_ps, 1)

            def output(g, b):
                i = 4 * g + b
                pe.wait_ge(ol_set, 2 * i + 2)
                pe.wait_ge(attwo_split, g + 1)
                wait(pe, x1_set, i)
                for t in range(2):
                    q = slice(t * P, (t + 1) * P)
                    for p in range(2):
                        w = slice(WQ + p * D, WQ + (p + 1) * D)
                        mm = three(psum[:, PJ + 1, t * D:(t + 1) * D], oT_hi[:, b % 2, p, q], oT_lo[:, b % 2, p, q],
                                   att_hi[:, g % 2, w], att_lo[:, g % 2, w], p == 0, p == 1)
                mm.then_inc(wo_ps, 1)

            norm_T(0)
            proj(0, 0, 0)
            proj(0, 0, 1)
            norm_T(1)
            qkT(0, 0)
            norm_T(2)
            norm_T(3)

            def step(g, b, has1, has2, more):
                nxt, prv = after(g, b), before(g, b)
                scores(g, b, 0)
                if more:
                    proj(*nxt, 0)
                    proj(*nxt, 1)
                if has1:
                    probT(*prv, 1)
                    value(*prv, 0)
                scores(g, b, 1)
                if more:
                    qkT(*nxt)
                if has1:
                    value(*prv, 1)
                probT(g, b, 0)
                if has2:
                    output(*before(*prv))

            run_steps(pe, step)
            last = (KV - 1, B - 1)
            probT(*last, 1)
            value(*last, 0)
            norm_T(4)
            value(*last, 1)
            output(*before(*last))
            norm_T(5)
            output(*last)

            def router():
                pe.wait_ge(pre_pool, 3)
                pe.wait_ge(x1_set, 4 * KV)
                for hf in range(2):
                    tok = slice(hf * 512, (hf + 1) * 512)
                    for k in range(KD):
                        w = wg2[:, k, :, :].rearrange("p a e -> p (a e)")
                        pe.matmul(psum[0:2 * E, LOGT_BANK[hf], :], w, actT_hi[:, k, tok], start=k == 0, stop=False)
                        mm = pe.matmul(psum[0:2 * E, LOGT_BANK[hf], :], w, actT_lo[:, k, tok],
                                       start=False, stop=k == KD - 1)
                mm.then_inc(logit_ps, 1)

            def router_T():
                pe.wait_ge(logT_set, 1)
                for tile in range(NT):
                    mm = pe.transpose(psum[:, LOGIT_BANK, tile * 2 * E:(tile + 1) * 2 * E],
                                      logT[:, tile * P:(tile + 1) * P], sm[0:2 * E, SMALL["ident"]:SMALL["ident"] + 2 * E])
                mm.then_inc(logitT_ps, 1)

            def up(e, par, hf, q):
                u = 4 * e + 2 * hf + q
                if hf == 0 and q == 0:
                    pe.wait_ge(expw_split, e + 1)
                if isinstance(u, int) and u == 0:
                    pe.wait_ge(hl_set, B + 2)
                wait(pe, prod_set, u - 1)
                tok = slice(hf * 512, (hf + 1) * 512)
                for w, s in ((0, up1_ps), (1, up3_ps)):
                    for k in range(KD):
                        c = slice((w * KD + k) * D + q * P, (w * KD + k) * D + (q + 1) * P)
                        mm = three(psum[:, 2 * q + w, :], exp_hi[:, par, c], exp_lo[:, par, c],
                                   actT_hi[:, k, tok], actT_lo[:, k, tok], k == 0, k == KD - 1)
                    mm.then_inc(s, 1)

            def down(e, par, hf):
                j = 2 * e + hf
                pe.wait_ge(al_set, 2 * j + 2)
                if isinstance(j, int) and j == 0:
                    pe.wait_ge(logit_set, 1)
                for c in range(2):
                    wait(pe, acc_set, 2 * j - 3 + c)
                    for tt in range(2):
                        tok = slice((2 * c + tt) * P, (2 * c + tt + 1) * P)
                        for q in range(2):
                            w = slice((2 * KD + q) * D, (2 * KD + q + 1) * D)
                            mm = three(psum[:, 4 + 2 * hf + c, tt * D:(tt + 1) * D],
                                       aT_hi[:, hf, q, tok], aT_lo[:, hf, q, tok],
                                       exp_hi[:, par, w], exp_lo[:, par, w], q == 0, q == 1)
                    mm.then_inc(down_ps, 1)

            def halves(ep, first):
                for par in range(2):
                    e = 2 * ep + par
                    for hf in range(2):
                        up(e, par, hf, 0)
                        if first and par == 0 and hf == 1:
                            router_T()
                        if first and par == 0 and hf == 0:
                            norm_T(6)
                            norm_T(7)
                        up(e, par, hf, 1)
                        if first and par == 0 and hf == 0:
                            pe.wait_ge(hl_set, 2 * B)
                            router()
                        if hf:
                            down(e, par, 0)
                        elif par:
                            down(e - 1, 0, 1)
                        elif not first:
                            down(e - 1, 1, 1)

            halves(0, True)
            with pe.Fori(1, E // 2) as ep:
                halves(ep, False)
            down(E - 1, 1, 1)

        @block.scalar
        def _(act):
            def colsum(b):
                act.wait_ge(x_in[b], 16)
                for k in range(KD):
                    tok = slice(b * S, (b + 1) * S)
                    ins = act.activation(hT_hi[:, k, tok], xTs[:, k, tok], ACT.Copy,
                                         accum_out=vsum[:, b, k:k + 1])
                ins.then_inc(xsum_set, 1)

            def cond_hi(b):
                tok = slice(b * S, (b + 1) * S)
                act.wait_ge(vq_set, b + 1)
                for k in range(KD):
                    ins = act.activation(actT_hi[:, k, tok], xTs[:, k, tok], ACT.Identity,
                                         scale=qs[:, k, b:b + 1], bias=vq[:, b, k:k + 1])
                ins.then_inc(xqh_set, 1)

            def squares(n):
                b = n % B
                for t in range(2):
                    ins = act.activation(junk[:, t, :], y[:, 2 * b + t, :], ACT.Square,
                                         accum_out=ss[:, n // B, 2 * b + t:2 * b + t + 1])
                ins.then_inc(sq_set, 1)

            def root(n):
                b = n % B
                c = (slice(None), n // B, slice(2 * b, 2 * b + 2))
                act.wait_ge(sq_set, n + 1)
                act.activation(rstd[c], ss[c], ACT.Sqrt, scale=1.0 / D, bias=eps[:, :]).then_inc(std_set, 1)

            def norm_hi(n):
                b = n % B
                tok = slice(b * S, (b + 1) * S)
                dst = hT_hi if n < B else actT_hi
                w = SMALL["ln"] if n < B else SMALL["ffln"]
                act.wait_ge(hnT_ps, n + 1)
                for k in range(KD):
                    ins = act.activation(dst[:, k, tok], psum[:, NORM_BANK[n], k * S:(k + 1) * S], ACT.Copy,
                                         scale=sm[:, w + k:w + k + 1])
                ins.then_inc(hh_set, 1)

            def cond_out(b):
                act.wait_ge(cond_ps, b + 1)
                act.activation(y[:, 2 * b:2 * b + 2, :], psum[:, b, :].rearrange("p (t d) -> p t d", t=2),
                               ACT.Relu).then_inc(y_set, 1)
                act.wait_ge(y_set, b + 1)

            act.wait_ge(ones_set, 3)
            act.activation(root_eps[:, :], eps[:, :], ACT.Sqrt)
            colsum(0)
            colsum(1)
            cond_hi(0)
            colsum(2)
            cond_hi(1)
            colsum(3)
            cond_hi(2)
            cond_hi(3)
            cond_out(0)
            squares(0)
            root(0)
            cond_out(1)
            squares(1)
            root(1)
            act.wait_ge(small_in, 16)
            norm_hi(0)
            cond_out(2)
            squares(2)
            root(2)
            cond_out(3)
            squares(3)
            root(3)
            norm_hi(1)
            act.activation(ident_bf[:, :], ident, ACT.Copy).then_inc(consts_set, 1)

            def exps(g, b, p):
                m = 2 * (4 * g + b) + p
                act.wait_ge(max_set, m + 1)
                wait(act, pT_ps, m - 1)
                for t in range(2):
                    c = slice(t * P, t * P + (t + 1) * P)
                    for h in range(2):
                        ins = act.activation(prob[:, p, h, c], psum[:, S_BANK + h, c], ACT.Exp,
                                             bias=nmax[:, p, t, h:h + 1], accum_out=rsum[:, p, t, h:h + 1])
                ins.then_inc(exp_set, 1)

            def probT_hi(g, b, p):
                m = 2 * (4 * g + b) + p
                act.wait_ge(pT_ps, m + 1)
                wait(act, pv_ps, m - 1)
                act.activation(pT_hi[:, p, :, :], psum[:, PT_BANK:PT_BANK + 2, 0:3 * P], ACT.Copy)\
                   .then_inc(pTh_set, 1)

            def value_hi(g, b, p):
                i = 4 * g + b
                act.wait_ge(pv_ps, 2 * i + p + 1)
                wait(act, wo_ps, i - 1)
                for h in range(2):
                    r = slice(h * HD, (h + 1) * HD)
                    ins = act.activation(oT_hi[r, b % 2, p, :], psum[r, PV, h * S:(h + 1) * S], ACT.Copy)
                ins.then_inc(oh_set, 1)

            def qk_hi(g, b):
                i = 4 * g + b
                act.wait_ge(qkT_ps, i + 1)
                act.activation(qT_hi[:, :, :], psum[:, QT, :].rearrange("p (a s) -> p a s", a=2), ACT.Copy)
                act.activation(kT_hi[:, :], psum[:, PJ, 0:S], ACT.Copy).then_inc(qkh_set, 1)

            def residual_root(n):
                act.wait_ge(x1_set, 4 * (KV - 1) + n - B + 1)
                squares(n)
                root(n)

            qk_hi(0, 0)
            norm_hi(2)
            norm_hi(3)

            def step(g, b, has1, has2, more):
                prv = before(g, b)
                exps(g, b, 0)
                if has1:
                    probT_hi(*prv, 1)
                    value_hi(*prv, 0)
                if more:
                    qk_hi(*after(g, b))
                exps(g, b, 1)
                if not more:
                    residual_root(4)
                if has1:
                    value_hi(*prv, 1)
                probT_hi(g, b, 0)

            run_steps(act, step)
            probT_hi(KV - 1, B - 1, 1)
            value_hi(KV - 1, B - 1, 0)
            residual_root(5)
            value_hi(KV - 1, B - 1, 1)
            norm_hi(4)
            residual_root(6)
            norm_hi(5)
            residual_root(7)
            norm_hi(6)
            norm_hi(7)

            def unit(e, hf, q):
                u = 4 * e + 2 * hf + q
                j = 2 * e + hf
                act.wait_ge(up1_ps, u + 1)
                wait(act, prod_set, u - 1)
                act.activation(sil[:, q, :], psum[:, 2 * q, :], ACT.Silu).then_inc(sil_set, 1)
                act.wait_ge(prod_set, u + 1)
                wait(act, down_ps, 2 * j - 2)
                act.activation(aT_hi[:, hf, q, :], prod[:, q, :], ACT.Copy).then_inc(ah_set, 1)

            unit(0, 0, 0)
            unit(0, 0, 1)
            act.wait_ge(logit_ps, 1)
            for hf in range(2):
                ins = act.activation(logT[:, hf * 512:(hf + 1) * 512], psum[0:2 * E, LOGT_BANK[hf], :], ACT.Copy)
            ins.then_inc(logT_set, 1)
            unit(0, 1, 0)
            act.wait_ge(lshift, 1)
            act.activation(expl[:, :, :], expl[:, :, :], ACT.Exp).then_inc(lexp, 1)
            unit(0, 1, 1)
            with act.Fori(1, E) as e:
                for hf in range(2):
                    for q in range(2):
                        unit(e, hf, q)

        @block.vector
        def _(dve):
            count = [0]

            def chain(ins):
                count[0] += 1
                ins.then_inc(pre_dve, 1)
                dve.wait_ge(pre_dve, count[0])

            dve.memset(ones[:, :], 1.0).then_inc(ones_set, 1)
            dve.memset(eps[:, :], EPS).then_inc(ones_set, 1)
            dve.memset(logit[:, :, E:E + 4], BIG).then_inc(ones_set, 1)
            dve.wait_ge(qemb_ps, 1)
            for k in range(KD):
                chain(dve.tensor_scalar(qemb[:, k, :], psum[:, 4, k * B:(k + 1) * B],
                                        sm[:, SMALL["b3"] + k:SMALL["b3"] + k + 1], 0.0, ALU.add, ALU.max))
            chain(dve.tensor_scalar(qs[:, :, :], qemb[:, :, :], float(S), None, ALU.mult))

            def cond_in_sum(b):
                tok = slice(b * S, (b + 1) * S)
                dve.wait_ge(xsum_set, b + 1)
                dve.tensor_tensor(vq[:, b, :], vsum[:, b, :], qemb[:, :, b], ALU.mult).then_inc(vq_set, 1)
                for k in range(KD):
                    ins = dve.tensor_scalar(xa[:, k, tok], xTs[:, k, tok], float(S), vsum[:, b, k:k + 1],
                                            ALU.mult, ALU.add)
                chain(ins)

            def cond_lo(b):
                tok = slice(b * S, (b + 1) * S)
                dve.wait_ge(xqh_set, b + 1)
                for k in range(KD):
                    ins = dve.scalar_tensor_tensor(out=actT_lo[:, k, tok], in0=xa[:, k, tok],
                                                   scalar=qemb[:, k, b:b + 1],
                                                   in1=actT_hi[:, k, tok].bitcast(F32),
                                                   op0=ALU.mult, op1=ALU.subtract)
                ins.then_inc(xql_set, 1)

            cond_in_sum(0)
            cond_in_sum(1)
            cond_lo(0)
            cond_in_sum(2)
            cond_lo(1)
            cond_in_sum(3)
            cond_lo(2)
            cond_lo(3)

            def normed(n):
                b = n % B
                c = (slice(None), n // B, slice(2 * b, 2 * b + 2))
                dve.wait_ge(sq_set, n + 1)
                dve.tensor_scalar(var[c], ss[c], 1.0 / D, EPS, ALU.mult, ALU.add)
                dve.wait_ge(std_set, n + 1)
                chain(dve.reciprocal(rstd[c], rstd[c]))
                chain(dve.scalar_tensor_tensor(out=nt1[c], in0=rstd[c], scalar=-0.5, in1=rstd[c],
                                               op0=ALU.mult, op1=ALU.mult))
                chain(dve.tensor_tensor(nt1[c], nt1[c], var[c], ALU.mult))
                chain(dve.scalar_tensor_tensor(out=rstd[c], in0=nt1[c], scalar=1.5, in1=rstd[c],
                                               op0=ALU.add, op1=ALU.mult))
                wait(dve, hnT_ps, n - 1)
                for t in range(2):
                    ins = dve.tensor_scalar(hn[:, n % 2, t, :], y[:, 2 * b + t, :],
                                            rstd[:, n // B, 2 * b + t:2 * b + t + 1], None, ALU.mult)
                ins.then_inc(hn_set, 1)

            def norm_lo(n):
                b = n % B
                tok = slice(b * S, (b + 1) * S)
                hi, lo = (hT_hi, hT_lo) if n < B else (actT_hi, actT_lo)
                w = SMALL["ln"] if n < B else SMALL["ffln"]
                dve.wait_ge(hh_set, n + 1)
                for k in range(KD):
                    ins = dve.scalar_tensor_tensor(out=lo[:, k, tok], in0=psum[:, NORM_BANK[n], k * S:(k + 1) * S],
                                                   scalar=sm[:, w + k:w + k + 1],
                                                   in1=hi[:, k, tok].bitcast(F32),
                                                   op0=ALU.mult, op1=ALU.subtract)
                ins.then_inc(hl_set, 1)

            normed(0)
            normed(1)
            norm_lo(0)
            normed(2)

            def columns(g, b, t):
                i = 4 * g + b
                dve.wait_ge(proj_ps, 2 * i + t + 1)
                if isinstance(g, int) and g == 0 and b == 0 and t == 0:
                    dve.wait_ge(rope_in, 16)
                wait(dve, rope_add, i)
                dve.tensor_tensor(rc[:, t, :], psum[:, PJ + t, 0:ROT], rope_sb[:, 0, t, :], ALU.mult)
                dve.tensor_tensor(rs_[:, t, :], psum[:, PJ + t, 0:ROT], rope_sb[:, 1, t, :], ALU.mult)\
                   .then_inc(rope_mul, 1)
                val = psum[:, PJ + t, None, ROT:QKV].to_broadcast([P, 2, HD])
                dve.tensor_copy(v_hi[:, b, t, :, :], val).then_inc(vh_set, 1)
                dve.wait_ge(vh_set, 2 * i + t + 1)
                dve.tensor_tensor(v_lo[:, b, t, :, :], val, v_hi[:, b, t, :, :].bitcast(F32),
                                  ALU.subtract).then_inc(vl_set, 1)

            def qk_lo(g, b):
                dve.wait_ge(qkh_set, 4 * g + b + 1)
                dve.tensor_tensor(qT_lo[:, :, :], psum[:, QT, :].rearrange("p (a s) -> p a s", a=2),
                                  qT_hi[:, :, :].bitcast(F32), ALU.subtract)
                dve.tensor_tensor(kT_lo[:, :], psum[:, PJ, 0:S], kT_hi[:, :].bitcast(F32), ALU.subtract)\
                   .then_inc(qkl_set, 1)

            def maxima(g, b, p):
                m = 2 * (4 * g + b) + p
                dve.wait_ge(score_ps, m + 1)
                for t in range(2):
                    ins = dve.tensor_reduce(nmax[:, p, t, :],
                                            psum[:, S_BANK:S_BANK + 2, t * P:t * P + (t + 1) * P],
                                            X, ALU.max, negate=True)
                ins.then_inc(max_set, 1)

            def inverse(g, b, p):
                dve.wait_ge(exp_set, 2 * (4 * g + b) + p + 1)
                dve.reciprocal(rinv[:, p, :, :], rsum[:, p, :, :]).then_inc(inv_set, 1)

            def probT_lo(g, b, p):
                dve.wait_ge(pTh_set, 2 * (4 * g + b) + p + 1)
                dve.tensor_tensor(pT_lo[:, p, :, :], psum[:, PT_BANK:PT_BANK + 2, 0:3 * P],
                                  pT_hi[:, p, :, :].bitcast(F32), ALU.subtract).then_inc(pTl_set, 1)

            def value_lo(g, b, p):
                dve.wait_ge(oh_set, 2 * (4 * g + b) + p + 1)
                for h in range(2):
                    r = slice(h * HD, (h + 1) * HD)
                    ins = dve.tensor_tensor(oT_lo[r, b % 2, p, :], psum[r, PV, h * S:(h + 1) * S],
                                            oT_hi[r, b % 2, p, :].bitcast(F32), ALU.subtract)
                ins.then_inc(ol_set, 1)

            def residual(g, b):
                dve.wait_ge(wo_ps, 4 * g + b + 1)
                yb = y[:, 2 * b:2 * b + 2, :]
                dve.tensor_tensor(yb, psum[:, PJ + 1, :].rearrange("p (t d) -> p t d", t=2), yb, ALU.add)\
                   .then_inc(x1_set, 1)

            columns(0, 0, 0)
            columns(0, 0, 1)
            norm_lo(1)
            normed(3)
            qk_lo(0, 0)
            norm_lo(2)
            norm_lo(3)

            def step(g, b, has1, has2, more):
                nxt, prv = after(g, b), before(g, b)
                maxima(g, b, 0)
                if more:
                    columns(*nxt, 0)
                    columns(*nxt, 1)
                inverse(g, b, 0)
                if has1:
                    probT_lo(*prv, 1)
                    value_lo(*prv, 0)
                maxima(g, b, 1)
                if more:
                    qk_lo(*nxt)
                inverse(g, b, 1)
                if has1:
                    value_lo(*prv, 1)
                probT_lo(g, b, 0)
                if not more:
                    normed(4)
                if has2:
                    residual(*before(*prv))

            run_steps(dve, step)
            probT_lo(KV - 1, B - 1, 1)
            value_lo(KV - 1, B - 1, 0)
            normed(5)
            value_lo(KV - 1, B - 1, 1)
            norm_lo(4)
            residual(KV - 1, B - 2)
            norm_lo(5)
            normed(6)
            residual(KV - 1, B - 1)
            normed(7)
            norm_lo(6)
            norm_lo(7)

            def shifted_logits():
                dve.wait_ge(logitT_ps, 1)
                lg = psum[:, LOGIT_BANK, 0:NT * 2 * E].rearrange("p (t a e) -> p t e a", t=NT, a=2)
                dve.tensor_reduce(logit[:, :, 0:E], lg, X, ALU.add).then_inc(logit_set, 1)
                dve.wait_ge(logit_set, 1)
                for tile in range(NT):
                    ins = dve.max(top[:, tile, :], logit[:, tile, 0:E])
                chain(ins)
                chain(dve.tensor_tensor(expl[:, :, :], logit[:, :, 0:E], top[:, :, 0:1].to_broadcast([P, NT, E]),
                                        ALU.subtract))
                dve.memset(top[:, :, TOPK:8], BIG).then_inc(lshift, 1)
                dve.wait_ge(lshift, 1)

            def choose():
                for tile in range(NT):
                    ins = dve.match_replace(left[:, tile, :], top[:, tile, :], logit[:, tile, :], -BIG)
                chain(ins)
                chain(dve.tensor_tensor(chosen[:, :, :], left[:, :, 0:E], logit[:, :, 0:E], ALU.not_equal))
                dve.wait_ge(lexp, 1)
                chain(dve.tensor_tensor(chosen[:, :, :], chosen[:, :, :], expl[:, :, :], ALU.mult))
                chain(dve.tensor_reduce(gsum[:, :], chosen[:, :, :], X, ALU.add))
                chain(dve.reciprocal(gsum[:, :], gsum[:, :]))
                chain(dve.tensor_tensor(gates[:, :, :], chosen[:, :, :],
                                        gsum[:, :, None].to_broadcast([P, NT, E]), ALU.mult))

            def product(e, hf, q):
                u = 4 * e + 2 * hf + q
                dve.wait_ge(sil_set, u + 1)
                dve.wait_ge(up3_ps, u + 1)
                wait(dve, ah_set, u - 1)
                dve.tensor_tensor(prod[:, q, :], psum[:, 2 * q + 1, :], sil[:, q, :], ALU.mult)\
                   .then_inc(prod_set, 1)
                dve.wait_ge(ah_set, u + 1)
                dve.tensor_tensor(aT_lo[:, hf, q, :], prod[:, q, :], aT_hi[:, hf, q, :].bitcast(F32),
                                  ALU.subtract).then_inc(al_set, 1)

            def accumulate(e, hf):
                j = 2 * e + hf
                for c in range(2):
                    dve.wait_ge(down_ps, 2 * j + c + 1)
                    for tt in range(2):
                        tile = 4 * hf + 2 * c + tt
                        ins = dve.scalar_tensor_tensor(out=y[:, tile, :],
                                                       in0=psum[:, 4 + 2 * hf + c, tt * D:(tt + 1) * D],
                                                       scalar=gates[:, tile, bass.ds(e, 1)], in1=y[:, tile, :],
                                                       op0=ALU.mult, op1=ALU.add)
                    ins.then_inc(acc_set, 1)

            def expert(e, first):
                for hf in range(2):
                    product(e, hf, 0)
                    if first and hf:
                        shifted_logits()
                    product(e, hf, 1)
                    if first and hf:
                        choose()
                        dve.wait_ge(xadd_set, 1)
                    if hf:
                        accumulate(e, 0)
                    elif not first:
                        accumulate(e - 1, 1)

            expert(0, True)
            with dve.Fori(1, E) as e:
                expert(e, False)
            accumulate(E - 1, 1)

        @block.gpsimd
        def _(pool):
            n_self = [0]

            def chain(ins):
                n_self[0] += 1
                ins.then_inc(pre_pool, 1)
                pool.wait_ge(pre_pool, n_self[0])

            def times_one(dst, src, shape):
                return pool.tensor_tensor(dst, src, ones[:, 0:1].to_broadcast(shape), ALU.mult)

            def split(hi, lo, raw, shape, hi_set, count):
                ones_n = ones[0:shape[0], 0:1] if len(shape) == 2 else ones[:, 0:1, None]
                pool.tensor_tensor(hi, raw, ones_n.to_broadcast(shape), ALU.mult).then_inc(hi_set, 1)
                pool.wait_ge(hi_set, count)
                return pool.tensor_tensor(lo, raw, hi.bitcast(F32), ALU.subtract)

            def split_proj(g):
                pool.wait_ge(attw_in, 16 * (g + 1))
                if not isinstance(g, int) or g > 1:
                    pool.wait_ge(proj_ps, 8 * (g - 1))
                split(att_hi[:, g % 2, 0:WQ], att_lo[:, g % 2, 0:WQ], att_raw[:, 0:WQ], [P, WQ], atth_set, 2 * g + 1)\
                    .then_inc(attw_split, 1)

            def split_out(g):
                if not isinstance(g, int) or g > 1:
                    pool.wait_ge(wo_ps, 4 * (g - 1))
                split(att_hi[:, g % 2, WQ:], att_lo[:, g % 2, WQ:], att_raw[:, WQ:], [P, WO], atth_set, 2 * g + 2)\
                    .then_inc(attwo_split, 1)

            pool.wait_ge(ones_set, 1)
            pool.wait_ge(cond_in, 48)
            pool.tensor_tensor(ones_r[:, :], ones[0:1, :], ones[0:1, :], ALU.mult)
            split(b2_parts[:, 0, :], b2_parts[:, 1, :], b2_sb[:, :], [1, 2 * D], w2h_set, 1).then_inc(w2_split, 1)
            pool.wait_ge(w2_in, 16)
            split(w2_hi[:, :, :], w2_lo[:, :, :], w2_raw[:, :, :], [P, KD, D], w2h_set, 2).then_inc(w2_split, 1)
            split_proj(0)
            split_out(0)
            wg = sm[:, SMALL["wg"]:SMALL["wg"] + KD * E].rearrange("p (k e) -> p k e", k=KD)
            pool.wait_ge(small_in, 16)
            chain(times_one(wg2[:, 0, 0, :], wg[:, 0, :], [P, E]))
            chain(times_one(wg2[:, 1, 0, :], wg[:, 1, :], [P, E]))
            chain(pool.tensor_tensor(wg2[:, :, 1, :], wg, wg2[:, :, 0, :].bitcast(F32), ALU.subtract))

            def rope(g, b):
                i = 4 * g + b
                wait(pool, qkT_ps, i)
                for t in range(2):
                    pool.wait_ge(rope_mul, 2 * i + t + 1)
                    c = rc[:, t, :].rearrange("p (h a e) -> p h a e", a=2, e=HD // 2)
                    s = rs_[:, t, :].rearrange("p (h a e) -> p h a e", a=2, e=HD // 2)
                    r = rot[:, t, :].rearrange("p (h a e) -> p h a e", a=2, e=HD // 2)
                    for a in range(2):
                        pool.tensor_tensor(r[:, 0:GH + 1, a, :], c[:, :, a, :], s[:, :, 1 - a, :], ALU.add)
                        ins = pool.tensor_tensor(r[:, GH + 1, a, :], c[:, GH, a, :], s[:, GH, 1 - a, :], ALU.add)
                ins.then_inc(rope_add, 1)

            def normalise(g, b, p):
                pool.wait_ge(inv_set, 2 * (4 * g + b) + p + 1)
                for t in range(2):
                    w = (t + 1) * P
                    pr = prob[:, p, :, t * P:t * P + w]
                    ins = pool.tensor_tensor(pr, pr, rinv[:, p, t, :, None].to_broadcast([P, 2, w]), ALU.mult)
                ins.then_inc(norm_set, 1)

            rope(0, 0)

            def step(g, b, has1, has2, more):
                if more:
                    rope(*after(g, b))
                normalise(g, b, 0)
                normalise(g, b, 1)
                if not (isinstance(g, int) and g == KV - 1):
                    if b == 1:
                        split_proj(g + 1)
                    elif b == 2:
                        split_out(g + 1)
                elif b % 2:
                    exp_split_lo(b // 2, b // 2)
                else:
                    exp_split_hi(b // 2, b // 2)

            def exp_split_hi(e, par):
                pool.wait_ge(expw_in[par], 16 * (e // 2 + 1) if isinstance(e, int) else 8 * (e - par) + 16)
                wait(pool, down_ps, 4 * (e - 1))
                times_one(exp_hi[:, par, :], exp_raw[:, par, :], [P, EW]).then_inc(exph_set, 1)

            def exp_split_lo(e, par):
                pool.wait_ge(exph_set, e + 1)
                pool.tensor_tensor(exp_lo[:, par, :], exp_raw[:, par, :], exp_hi[:, par, :].bitcast(F32),
                                   ALU.subtract).then_inc(expw_split, 1)

            run_steps(pool, step)
            pool.wait_ge(xn_in, 16)
            pool.wait_ge(hn_set, 2 * B)
            pool.tensor_tensor(y[:, :, :], y[:, :, :], x_sb[:, :, :], ALU.add).then_inc(xadd_set, 1)
            with pool.Fori(1, E // 2) as ep:
                for par in range(2):
                    exp_split_hi(2 * ep + par, par)
                    exp_split_lo(2 * ep + par, par)


def kernel(x, cond_1024, L0_cond_W3, L0_cond_b3, L0_cond_W2, L0_cond_b2, L0_ffn_ln_w, L0_ffn_ff_ln_w,
           L0_ffn_wq, L0_ffn_wk, L0_ffn_wv, L0_ffn_wo, L0_ffn_wg, L0_ffn_w1, L0_ffn_w3, L0_ffn_w2):
    import ml_dtypes
    import concourse.bacc as _bacc
    from concourse.bass_utils import run_bass_kernel_spmd as _run

    def a(v):
        return np.asarray(v)

    def cols(v):
        return a(v).reshape(KD, P).T

    def rows(w):
        w = a(w)
        return w.reshape(-1, P, w.shape[-1]).transpose(1, 0, 2)

    xf = a(x).reshape(B * S, D)
    small = np.concatenate([a(cond_1024).T, cols(L0_cond_b3), cols(L0_ffn_ln_w), cols(L0_ffn_ff_ln_w),
                            rows(L0_ffn_wg).reshape(P, KD * E), np.eye(P, dtype=np.float32)], axis=1)
    wq = rows(L0_ffn_wq).reshape(P, KD, KV, GH * HD)
    wk = rows(L0_ffn_wk).reshape(P, KD, KV, HD)
    wv = rows(L0_ffn_wv).reshape(P, KD, KV, HD)
    qkv = np.concatenate([wq, wk, wv], axis=3).transpose(2, 0, 1, 3).reshape(KV, P, WQ)
    wo = a(L0_ffn_wo).reshape(KV, 2, P, D).transpose(0, 2, 1, 3).reshape(KV, P, WO)
    attw = np.concatenate([qkv, wo], axis=2)
    expw = np.stack([a(w).reshape(E, KD, P, D).transpose(0, 2, 1, 3) for w in (L0_ffn_w1, L0_ffn_w3, L0_ffn_w2)],
                    axis=2).reshape(E, P, EW)
    half = HD // 2
    inv = (np.float32(1.0) / np.float32(150000.0) ** (np.arange(half, dtype=np.float32) / np.float32(half)))
    ang = np.arange(S, dtype=np.float32)[:, None] * inv.astype(np.float32)
    cos, sin = np.cos(ang), np.sin(ang)
    scale = np.array([HD ** -0.5] * GH + [1.0], np.float32)[None, :, None, None]
    tab = np.stack([np.stack([cos, cos], 1)[:, None] * scale, np.stack([sin, -sin], 1)[:, None] * scale])
    rope = tab.astype(np.float32).reshape(2, 2, P, ROT).transpose(2, 0, 1, 3)
    mask = np.triu(np.full((P, P), -1e30, np.float32), 1).astype(ml_dtypes.bfloat16)

    data = dict(small=small, w3=a(L0_cond_W3), w2c=a(L0_cond_W2), b2=a(L0_cond_b2).reshape(1, D), xT=xf.T,
                xn=xf, rope=rope, mask=mask, attw=attw, expw=expw)
    nc = _bacc.Bacc("TRN2", target_bir_lowering=False, num_devices=1)
    arrays, args = {}, {}
    for name, v in data.items():
        v = np.ascontiguousarray(v)
        arrays["in_" + name] = v
        args[name] = nc.dram_tensor("in_" + name, v.shape, mybir.dt.from_np(v.dtype), kind="ExternalInput").ap()
    res = nc.dram_tensor("res", (B * S, D), F32, kind="ExternalOutput").ap()
    build(nc, out=res, **args)
    r = _run(nc, [arrays], core_ids=[0])
    return r.results[0]["res"].reshape(B, S, D)
```

```python
from contextlib import ExitStack

import numpy as np
import concourse.bass as bass
from concourse import mybir
from concourse.alu_op_type import AluOpType as ALU

F32 = mybir.dt.float32
F32R = mybir.dt.float32r
BF16 = mybir.dt.bfloat16
ACT = mybir.ActivationFunctionType
X = mybir.AxisListType.X

P = 128
B, S, D = 4, 256, 256
NT = B * S // P
KD = D // P
HEADS, KV, HD = 32, 8, 64
GH = HEADS // KV
E, TOPK = 16, 4
EPS = 1e-5
QKV = GH * HD + 2 * HD
ROT = (GH + 1) * HD
WQ, WO = KD * QKV, 2 * D
EW = 3 * KD * D
BIG = 3.0e38
SMALL = dict(cond=0, b3=4, ln=6, ffln=8, wg=10, ident=42)
NSMALL = 170


def build(nc, small, w3, w2c, b2, xT, xn, rope, mask, attw, expw, out):
    with ExitStack() as outer:
        def sem(name):
            return outer.enter_context(nc.semaphore(name))

        def keep(name, shape, dt=F32):
            return outer.enter_context(nc.sbuf_tensor(name, shape, dt))

        sm = keep("sm", [P, NSMALL])
        ident = sm[:, SMALL["ident"]:SMALL["ident"] + P]
        ident_bf = keep("ident_bf", [P, P], BF16)
        mask_sb = keep("mask_sb", [P, P], BF16)
        ones = keep("ones", [P, P])
        y = keep("y", [P, NT, D])
        actT_hi = keep("actT_hi", [P, KD, B * S], F32R)
        actT_lo = keep("actT_lo", [P, KD, B * S], F32R)
        ss = keep("ss", [P, 2, NT])
        var = keep("var", [P, 2, NT])
        rstd = keep("rstd", [P, 2, NT])
        nt1 = keep("nt1", [P, 2, NT])
        hn = keep("hn", [P, 2, 2, D])
        junk = keep("junk", [P, 2, 2, D])
        exp_raw = keep("exp_raw", [P, 2, EW])
        wg2 = keep("wg2", [P, KD, 2, E], F32R)
        eps = keep("eps", [P, 1])
        root_eps = keep("root_eps", [P, 1])
        gates = keep("gates", [P, NT, E])
        psum = outer.enter_context(nc.psum_tensor("psum", [P, 8, 512], F32))

        att_raw = keep("att_raw", [P, WQ + WO])
        att_hi = keep("att_hi", [P, 2, WQ + WO], F32R)
        att_lo = keep("att_lo", [P, 2, WQ + WO], F32R)
        rope_sb = keep("rope_sb", [P, 2, 2, ROT])
        rc = keep("rc", [P, 2, ROT])
        rs_ = keep("rs_", [P, 2, ROT])
        rot = keep("rot", [P, 2, ROT + HD])
        qT_hi = keep("qT_hi", [P, 2, S], F32R)
        qT_lo = keep("qT_lo", [P, 2, S], F32R)
        kT_hi = keep("kT_hi", [P, S], F32R)
        kT_lo = keep("kT_lo", [P, S], F32R)
        v_hi = keep("v_hi", [P, B, 2, 2, HD], F32R)
        v_lo = keep("v_lo", [P, B, 2, 2, HD], F32R)
        prob = keep("prob", [P, 2, 2, 3 * P])
        pT_hi = keep("pT_hi", [P, 2, 2, 3 * P], F32R)
        pT_lo = keep("pT_lo", [P, 2, 2, 3 * P], F32R)
        nmax = keep("nmax", [P, 2, 2, 2])
        rsum = keep("rsum", [P, 2, 2, 2])
        rinv = keep("rinv", [P, 2, 2, 2])
        oT_hi = keep("oT_hi", [P, 2, 2, S], F32R)
        oT_lo = keep("oT_lo", [P, 2, 2, S], F32R)
        exp_hi = keep("exp_hi", [P, 2, EW], F32R)
        exp_lo = keep("exp_lo", [P, 2, EW], F32R)
        logT = keep("logT", [2 * E, B * S])
        logit = keep("logit", [P, NT, E + 4])
        top = keep("top", [P, NT, 8])
        left = keep("left", [P, NT, E + 4])
        chosen = keep("chosen", [P, NT, E])
        expl = keep("expl", [P, NT, E])
        gsum = keep("gsum", [P, NT])

        with ExitStack() as early:
            def etmp(name, shape, dt=F32):
                return early.enter_context(nc.sbuf_tensor(name, shape, dt))

            hT_hi = etmp("hT_hi", [P, KD, B * S], F32R)
            hT_lo = etmp("hT_lo", [P, KD, B * S], F32R)
            xTs = etmp("xTs", [P, KD, B * S])
            xa = etmp("xa", [P, KD, B * S])
            w3_sb = etmp("w3_sb", [P, D])
            w2_raw = etmp("w2_raw", [P, KD, D])
            w2_hi = etmp("w2_hi", [P, KD, D], F32R)
            w2_lo = etmp("w2_lo", [P, KD, D], F32R)
            b2_sb = etmp("b2_sb", [1, 2 * D])
            b2_parts = etmp("b2_parts", [1, 2, 2 * D], F32R)
            ones_r = etmp("ones_r", [1, P], F32R)
            vsum = etmp("vsum", [P, B, KD])
            vq = etmp("vq", [P, B, KD])
            qemb = etmp("qemb", [P, KD, B])
            qs = etmp("qs", [P, KD, B])

        with ExitStack() as late:
            def etmp(name, shape, dt=F32):
                return late.enter_context(nc.sbuf_tensor(name, shape, dt))

            x_sb = etmp("x_sb", [P, NT, D])
            sil = etmp("sil", [P, 2, 512])
            prod = etmp("prod", [P, 2, 512])
            aT_hi = etmp("aT_hi", [P, 2, 2, 512], F32R)
            aT_lo = etmp("aT_lo", [P, 2, 2, 512], F32R)

        small_in = sem("small_in")
        w3_in = sem("w3_in")
        b2_in = sem("b2_in")
        w2_in = sem("w2_in")
        x_in = [sem(f"x_in{b}") for b in range(B)]
        rope_in = sem("rope_in")
        mask_in = sem("mask_in")
        attw_in = sem("attw_in")
        expw_in = [sem("expw_in0"), sem("expw_in1")]
        xn_in = sem("xn_in")
        stored = sem("stored")
        consts_set = sem("consts_set")
        ones_set = sem("ones_set")
        qemb_ps = sem("qemb_ps")
        pre_dve = sem("pre_dve")
        w2h_set = sem("w2h_set")
        w2_split = sem("w2_split")
        pre_pool = sem("pre_pool")
        xsum_set = sem("xsum_set")
        vq_set = sem("vq_set")
        xqh_set = sem("xqh_set")
        xql_set = sem("xql_set")
        cond_ps = sem("cond_ps")
        y_set = sem("y_set")
        sq_set = sem("sq_set")
        std_set = sem("std_set")
        hn_set = sem("hn_set")
        hnT_ps = sem("hnT_ps")
        hh_set = sem("hh_set")
        hl_set = sem("hl_set")
        attw_split = sem("attw_split")
        attwo_split = sem("attwo_split")
        atth_set = sem("atth_set")
        proj_ps = sem("proj_ps")
        rope_mul = sem("rope_mul")
        vh_set = sem("vh_set")
        vl_set = sem("vl_set")
        rope_add = sem("rope_add")
        qkT_ps = sem("qkT_ps")
        qkh_set = sem("qkh_set")
        qkl_set = sem("qkl_set")
        score_ps = sem("score_ps")
        max_set = sem("max_set")
        exp_set = sem("exp_set")
        inv_set = sem("inv_set")
        norm_set = sem("norm_set")
        pT_ps = sem("pT_ps")
        pTh_set = sem("pTh_set")
        pTl_set = sem("pTl_set")
        pv_ps = sem("pv_ps")
        oh_set = sem("oh_set")
        ol_set = sem("ol_set")
        wo_ps = sem("wo_ps")
        x1_set = sem("x1_set")
        logit_ps = sem("logit_ps")
        logT_set = sem("logT_set")
        logitT_ps = sem("logitT_ps")
        xadd_set = sem("xadd_set")
        logit_set = sem("logit_set")
        lshift = sem("lshift")
        lexp = sem("lexp")
        expw_split = sem("expw_split")
        exph_set = sem("exph_set")
        up1_ps = sem("up1_ps")
        up3_ps = sem("up3_ps")
        sil_set = sem("sil_set")
        prod_set = sem("prod_set")
        ah_set = sem("ah_set")
        al_set = sem("al_set")
        down_ps = sem("down_ps")
        acc_set = sem("acc_set")

        block = outer.enter_context(nc.Block())

        PJ, QT, PV = 4, 6, 7
        S_BANK, PT_BANK = 0, 2
        NORM_BANK = (7, 3, 7, 3, 4, 6, 4, 6)
        LOGT_BANK, LOGIT_BANK = (7, 5), 4

        def before(g, b):
            return (g, b - 1) if b else (g - 1, B - 1)

        def after(g, b):
            return (g, b + 1) if b < B - 1 else (g + 1, 0)

        def run_steps(eng, step):
            for b in range(B):
                step(0, b, b >= 1, b >= 2, True)
            with eng.Fori(1, KV - 1) as g:
                for b in range(B):
                    step(g, b, True, True, True)
            for b in range(B):
                step(KV - 1, b, True, True, b < B - 1)

        def wait(eng, s, count):
            if not isinstance(count, int) or count > 0:
                eng.wait_ge(s, count)

        @block.sync
        def _(sp):
            sp.dma_start(sm[:, :], small).then_inc(small_in, 16)
            sp.dma_start(w3_sb[:, :], w3).then_inc(w3_in, 16)
            xv = xT.rearrange("(k p) (b s) -> b p k s", p=P, b=B)
            for b in range(B):
                sp.dma_start(xTs[:, :, b * S:(b + 1) * S], xv[b]).then_inc(x_in[b], 16)
                if b == 0:
                    sp.dma_start(w2_raw[:, :, :], w2c.rearrange("(k p) n -> p k n", p=P)).then_inc(w2_in, 16)
                    sp.dma_start(b2_sb[:, 0:D], b2).then_inc(b2_in, 16)
                    sp.dma_start(b2_sb[:, D:], b2).then_inc(b2_in, 16)
            sp.dma_start(att_raw[:, :], attw[0]).then_inc(attw_in, 16)
            sp.dma_start(rope_sb[:, :, :, :], rope).then_inc(rope_in, 16)
            sp.dma_start(mask_sb[:, :], mask).then_inc(mask_in, 16)
            for e in range(2):
                sp.dma_start(exp_raw[:, e, :], expw[e]).then_inc(expw_in[e], 16)
            with sp.Fori(1, KV) as g:
                sp.wait_ge(attwo_split, g)
                sp.dma_start(att_raw[:, :], attw[g]).then_inc(attw_in, 16)
            sp.wait_ge(proj_ps, 8 * KV)
            sp.dma_start(x_sb[:, :, :], xn.rearrange("(t p) d -> p t d", p=P)).then_inc(xn_in, 16)
            with sp.Fori(1, E // 2) as ep:
                for par in range(2):
                    sp.wait_ge(expw_split, 2 * ep + par - 1)
                    sp.dma_start(exp_raw[:, par, :], expw[2 * ep + par]).then_inc(expw_in[par], 16)
            ov = out.rearrange("(t p) d -> p t d", p=P)
            for c in range(4):
                sp.wait_ge(acc_set, 4 * (E - 1) + c + 1)
                sp.dma_start(ov[:, 2 * c:2 * c + 2, :], y[:, 2 * c:2 * c + 2, :]).then_inc(stored, 16)
            sp.wait_ge(stored, 64)

        @block.tensor
        def _(pe):
            def three(out_ap, sh, sl, mh, ml, start, stop):
                pe.matmul(out_ap, sh, mh, start=start, stop=False)
                pe.matmul(out_ap, sh, ml, start=False, stop=False)
                return pe.matmul(out_ap, sl, mh, start=False, stop=stop)

            pe.wait_ge(small_in, 16)
            pe.wait_ge(w3_in, 16)
            for k in range(KD):
                mm = pe.matmul(psum[:, 4, k * B:(k + 1) * B], w3_sb[:, k * P:(k + 1) * P],
                               sm[:, 0:B], start=True, stop=True)
            mm.then_inc(qemb_ps, 1)

            def cond_product(b):
                pe.wait_ge(w2_split, 1)
                pe.wait_ge(xql_set, b + 1)
                for t in range(2):
                    tok = slice(b * S + t * P, b * S + (t + 1) * P)
                    for k in range(KD):
                        three(psum[:, b, t * D:(t + 1) * D], actT_hi[:, k, tok], actT_lo[:, k, tok],
                              w2_hi[:, k, :], w2_lo[:, k, :], t == 0 and k == 0, False)
                pe.wait_ge(w2_split, 2)
                for part in range(2):
                    mm = pe.matmul(psum[:, b, :], ones_r[0:1, :], b2_parts[:, part, :], start=False, stop=part == 1)
                mm.then_inc(cond_ps, 1)

            def norm_T(n):
                pe.wait_ge(hn_set, n + 1)
                if n % B >= 2:
                    pe.wait_ge(hl_set, n - 1)
                elif n == 1:
                    pe.wait_ge(y_set, B)
                for k in range(KD):
                    for t in range(2):
                        mm = pe.transpose(psum[:, NORM_BANK[n], k * S + t * P:k * S + (t + 1) * P],
                                          hn[:, n % 2, t, k * P:(k + 1) * P], ident)
                mm.then_inc(hnT_ps, 1)

            def proj(g, b, t):
                i = 4 * g + b
                if t == 0:
                    pe.wait_ge(attw_split, g + 1)
                    wait(pe, qkl_set, i)
                else:
                    wait(pe, x1_set, i - 3)
                if isinstance(g, int) and g == 0:
                    pe.wait_ge(hl_set, b + 1)
                tok = slice(b * S + t * P, b * S + (t + 1) * P)
                for k in range(KD):
                    w = slice(k * QKV, (k + 1) * QKV)
                    mm = three(psum[:, PJ + t, 0:QKV], hT_hi[:, k, tok], hT_lo[:, k, tok],
                               att_hi[:, g % 2, w], att_lo[:, g % 2, w], k == 0, k == KD - 1)
                mm.then_inc(proj_ps, 1)

            def qkT(g, b):
                i = 4 * g + b
                pe.wait_ge(rope_add, i + 1)
                pe.wait_ge(vl_set, i + 1)
                for p in range(2):
                    for t in range(2):
                        pe.transpose(psum[:, QT, p * S + t * P:p * S + (t + 1) * P],
                                     rot[:, t, p * P:(p + 1) * P], ident)
                for t in range(2):
                    mm = pe.transpose(psum[:, PJ, t * P:(t + 1) * P], rot[:, t, 2 * P:3 * P], ident)
                mm.then_inc(qkT_ps, 1)

            def scores(g, b, p):
                i = 4 * g + b
                m = 2 * i + p
                pe.wait_ge(qkl_set, i + 1)
                wait(pe, exp_set, m)
                if isinstance(g, int) and g == 0 and b == 0 and p == 0:
                    pe.wait_ge(mask_in, 16)
                    pe.wait_ge(consts_set, 1)
                for t in range(2):
                    keys, cols = slice(0, (t + 1) * P), slice(t * P, t * P + (t + 1) * P)
                    q = slice(t * P, (t + 1) * P)
                    for n, (qs, ks) in enumerate(((qT_hi, kT_hi), (qT_hi, kT_lo), (qT_lo, kT_hi))):
                        for h in range(2):
                            r = slice(h * HD, (h + 1) * HD)
                            pe.matmul(psum[:, S_BANK + h, cols], qs[r, p, q], ks[r, keys],
                                      start=n == 0, stop=False)
                    for h in range(2):
                        mm = pe.matmul(psum[:, S_BANK + h, 2 * t * P:(2 * t + 1) * P], ident_bf[:, :],
                                       mask_sb[:, :], start=False, stop=True)
                mm.then_inc(score_ps, 1)

            def probT(g, b, p):
                m = 2 * (4 * g + b) + p
                pe.wait_ge(norm_set, m + 1)
                wait(pe, pTl_set, m)
                if isinstance(g, int) and m == 0:
                    pe.wait_ge(hl_set, B)
                for h in range(2):
                    for blk in range(3):
                        mm = pe.transpose(psum[:, PT_BANK + h, blk * P:(blk + 1) * P],
                                          prob[:, p, h, blk * P:(blk + 1) * P], ident)
                mm.then_inc(pT_ps, 1)

            def value(g, b, p):
                m = 2 * (4 * g + b) + p
                pe.wait_ge(pTl_set, m + 1)
                wait(pe, ol_set, m)
                pv = psum[:, PV, :].rearrange("p (h s) -> p h s", h=2)
                for kt in range(2):
                    pt = slice(2 * kt * P, 2 * kt * P + S - kt * P)
                    mm = three(pv[:, :, kt * P:S],
                               v_hi[:, b, kt, :, :].rearrange("p a e -> p (a e)"),
                               v_lo[:, b, kt, :, :].rearrange("p a e -> p (a e)"),
                               pT_hi[:, p, :, pt], pT_lo[:, p, :, pt], kt == 0, kt == 1)
                mm.then_inc(pv_ps, 1)

            def output(g, b):
                i = 4 * g + b
                pe.wait_ge(ol_set, 2 * i + 2)
                pe.wait_ge(attwo_split, g + 1)
                wait(pe, x1_set, i)
                for t in range(2):
                    q = slice(t * P, (t + 1) * P)
                    for p in range(2):
                        w = slice(WQ + p * D, WQ + (p + 1) * D)
                        mm = three(psum[:, PJ + 1, t * D:(t + 1) * D], oT_hi[:, b % 2, p, q], oT_lo[:, b % 2, p, q],
                                   att_hi[:, g % 2, w], att_lo[:, g % 2, w], p == 0, p == 1)
                mm.then_inc(wo_ps, 1)

            cond_product(0)
            cond_product(1)
            cond_product(2)
            norm_T(0)
            cond_product(3)
            proj(0, 0, 0)
            proj(0, 0, 1)
            norm_T(1)
            qkT(0, 0)
            norm_T(2)
            norm_T(3)

            def step(g, b, has1, has2, more):
                nxt, prv = after(g, b), before(g, b)
                scores(g, b, 0)
                if more:
                    proj(*nxt, 0)
                    proj(*nxt, 1)
                if has1:
                    probT(*prv, 1)
                    value(*prv, 0)
                scores(g, b, 1)
                if more:
                    qkT(*nxt)
                if has2:
                    output(*before(*prv))
                if has1:
                    value(*prv, 1)
                probT(g, b, 0)

            run_steps(pe, step)
            last = (KV - 1, B - 1)
            probT(*last, 1)
            value(*last, 0)
            norm_T(4)
            output(*before(*last))
            value(*last, 1)
            norm_T(5)
            output(*last)

            def router():
                pe.wait_ge(pre_pool, 3)
                pe.wait_ge(x1_set, 4 * KV)
                for hf in range(2):
                    tok = slice(hf * 512, (hf + 1) * 512)
                    for k in range(KD):
                        w = wg2[:, k, :, :].rearrange("p a e -> p (a e)")
                        pe.matmul(psum[0:2 * E, LOGT_BANK[hf], :], w, actT_hi[:, k, tok], start=k == 0, stop=False)
                        mm = pe.matmul(psum[0:2 * E, LOGT_BANK[hf], :], w, actT_lo[:, k, tok],
                                       start=False, stop=k == KD - 1)
                mm.then_inc(logit_ps, 1)

            def router_T():
                pe.wait_ge(logT_set, 1)
                for tile in range(NT):
                    mm = pe.transpose(psum[:, LOGIT_BANK, tile * 2 * E:(tile + 1) * 2 * E],
                                      logT[:, tile * P:(tile + 1) * P], ident[0:2 * E, 0:2 * E])
                mm.then_inc(logitT_ps, 1)

            def up(e, par, hf, q):
                u = 4 * e + 2 * hf + q
                if hf == 0 and q == 0:
                    pe.wait_ge(expw_split, e + 1)
                if isinstance(u, int) and u == 0:
                    pe.wait_ge(hl_set, B + 2)
                wait(pe, prod_set, u - 1)
                tok = slice(hf * 512, (hf + 1) * 512)
                for w, s in ((0, up1_ps), (1, up3_ps)):
                    for k in range(KD):
                        c = slice((w * KD + k) * D + q * P, (w * KD + k) * D + (q + 1) * P)
                        mm = three(psum[:, 2 * q + w, :], exp_hi[:, par, c], exp_lo[:, par, c],
                                   actT_hi[:, k, tok], actT_lo[:, k, tok], k == 0, k == KD - 1)
                    mm.then_inc(s, 1)

            def down(e, par, hf):
                j = 2 * e + hf
                pe.wait_ge(al_set, 2 * j + 2)
                if isinstance(j, int) and j == 0:
                    pe.wait_ge(logit_set, 1)
                for c in range(2):
                    wait(pe, acc_set, 2 * j - 3 + c)
                    for tt in range(2):
                        tok = slice((2 * c + tt) * P, (2 * c + tt + 1) * P)
                        for q in range(2):
                            w = slice((2 * KD + q) * D, (2 * KD + q + 1) * D)
                            mm = three(psum[:, 4 + 2 * hf + c, tt * D:(tt + 1) * D],
                                       aT_hi[:, hf, q, tok], aT_lo[:, hf, q, tok],
                                       exp_hi[:, par, w], exp_lo[:, par, w], q == 0, q == 1)
                    mm.then_inc(down_ps, 1)

            def halves(ep, first):
                for par in range(2):
                    e = 2 * ep + par
                    for hf in range(2):
                        up(e, par, hf, 0)
                        if first and par == 0 and hf == 1:
                            router_T()
                        if first and par == 0 and hf == 0:
                            norm_T(6)
                            norm_T(7)
                        up(e, par, hf, 1)
                        if first and par == 0 and hf == 0:
                            pe.wait_ge(hl_set, 2 * B)
                            router()
                        if hf:
                            down(e, par, 0)
                        elif par:
                            down(e - 1, 0, 1)
                        elif not first:
                            down(e - 1, 1, 1)

            halves(0, True)
            with pe.Fori(1, E // 2) as ep:
                halves(ep, False)
            down(E - 1, 1, 1)

        @block.scalar
        def _(act):
            def colsum(b):
                act.wait_ge(x_in[b], 16)
                for k in range(KD):
                    tok = slice(b * S, (b + 1) * S)
                    ins = act.activation(hT_hi[:, k, tok], xTs[:, k, tok], ACT.Copy,
                                         accum_out=vsum[:, b, k:k + 1])
                ins.then_inc(xsum_set, 1)

            def cond_hi(b):
                tok = slice(b * S, (b + 1) * S)
                act.wait_ge(vq_set, b + 1)
                for k in range(KD):
                    ins = act.activation(actT_hi[:, k, tok], xTs[:, k, tok], ACT.Identity,
                                         scale=qs[:, k, b:b + 1], bias=vq[:, b, k:k + 1])
                ins.then_inc(xqh_set, 1)

            def squares(n):
                b = n % B
                for t in range(2):
                    ins = act.activation(junk[:, n % 2, t, :], y[:, 2 * b + t, :], ACT.Square,
                                         accum_out=ss[:, n // B, 2 * b + t:2 * b + t + 1])
                ins.then_inc(sq_set, 1)

            def root(n):
                b = n % B
                c = (slice(None), n // B, slice(2 * b, 2 * b + 2))
                act.wait_ge(sq_set, n + 1)
                act.activation(rstd[c], ss[c], ACT.Sqrt, scale=1.0 / D, bias=eps[:, :]).then_inc(std_set, 1)

            def norm_hi(n):
                b = n % B
                tok = slice(b * S, (b + 1) * S)
                dst = hT_hi if n < B else actT_hi
                w = SMALL["ln"] if n < B else SMALL["ffln"]
                act.wait_ge(hnT_ps, n + 1)
                for k in range(KD):
                    ins = act.activation(dst[:, k, tok], psum[:, NORM_BANK[n], k * S:(k + 1) * S], ACT.Copy,
                                         scale=sm[:, w + k:w + k + 1])
                ins.then_inc(hh_set, 1)

            def cond_out(b):
                act.wait_ge(cond_ps, b + 1)
                act.activation(y[:, 2 * b:2 * b + 2, :], psum[:, b, :].rearrange("p (t d) -> p t d", t=2),
                               ACT.Relu).then_inc(y_set, 1)
                act.wait_ge(y_set, b + 1)

            act.wait_ge(ones_set, 3)
            act.activation(root_eps[:, :], eps[:, :], ACT.Sqrt)
            colsum(0)
            colsum(1)
            cond_hi(0)
            colsum(2)
            cond_hi(1)
            colsum(3)
            cond_hi(2)
            cond_hi(3)
            cond_out(0)
            squares(0)
            root(0)
            cond_out(1)
            squares(1)
            root(1)
            act.wait_ge(small_in, 16)
            norm_hi(0)
            cond_out(2)
            squares(2)
            root(2)
            cond_out(3)
            squares(3)
            root(3)
            norm_hi(1)
            act.activation(ident_bf[:, :], ident, ACT.Copy).then_inc(consts_set, 1)

            def exps(g, b, p):
                m = 2 * (4 * g + b) + p
                act.wait_ge(max_set, m + 1)
                wait(act, pT_ps, m - 1)
                for t in range(2):
                    c = slice(t * P, t * P + (t + 1) * P)
                    for h in range(2):
                        ins = act.activation(prob[:, p, h, c], psum[:, S_BANK + h, c], ACT.Exp,
                                             bias=nmax[:, p, t, h:h + 1], accum_out=rsum[:, p, t, h:h + 1])
                ins.then_inc(exp_set, 1)

            def probT_hi(g, b, p):
                m = 2 * (4 * g + b) + p
                act.wait_ge(pT_ps, m + 1)
                wait(act, pv_ps, m - 1)
                act.activation(pT_hi[:, p, :, :], psum[:, PT_BANK:PT_BANK + 2, 0:3 * P], ACT.Copy)\
                   .then_inc(pTh_set, 1)

            def value_hi(g, b, p):
                i = 4 * g + b
                act.wait_ge(pv_ps, 2 * i + p + 1)
                wait(act, wo_ps, i - 1)
                for h in range(2):
                    r = slice(h * HD, (h + 1) * HD)
                    ins = act.activation(oT_hi[r, b % 2, p, :], psum[r, PV, h * S:(h + 1) * S], ACT.Copy)
                ins.then_inc(oh_set, 1)

            def values_hi(g, b):
                i = 4 * g + b
                act.wait_ge(rope_mul, 2 * i + 2)
                for t in range(2):
                    ins = act.activation(v_hi[:, b, t, :, :],
                                         psum[:, PJ + t, None, ROT:QKV].to_broadcast([P, 2, HD]), ACT.Copy)
                ins.then_inc(vh_set, 1)

            def qk_hi(g, b):
                i = 4 * g + b
                act.wait_ge(qkT_ps, i + 1)
                act.activation(qT_hi[:, :, :], psum[:, QT, :].rearrange("p (a s) -> p a s", a=2), ACT.Copy)
                act.activation(kT_hi[:, :], psum[:, PJ, 0:S], ACT.Copy).then_inc(qkh_set, 1)

            def residual_squares(n):
                act.wait_ge(x1_set, 4 * (KV - 1) + n - B + 1)
                squares(n)

            values_hi(0, 0)
            qk_hi(0, 0)
            norm_hi(2)
            norm_hi(3)

            def step(g, b, has1, has2, more):
                prv = before(g, b)
                exps(g, b, 0)
                if more:
                    values_hi(*after(g, b))
                if has1:
                    probT_hi(*prv, 1)
                    value_hi(*prv, 0)
                if more:
                    qk_hi(*after(g, b))
                if not more:
                    residual_squares(4)
                exps(g, b, 1)
                if has1:
                    value_hi(*prv, 1)
                probT_hi(g, b, 0)

            run_steps(act, step)
            root(4)
            probT_hi(KV - 1, B - 1, 1)
            value_hi(KV - 1, B - 1, 0)
            residual_squares(5)
            root(5)
            norm_hi(4)
            value_hi(KV - 1, B - 1, 1)
            residual_squares(6)
            root(6)
            norm_hi(5)
            residual_squares(7)
            root(7)
            norm_hi(6)
            norm_hi(7)

            def unit(e, hf, q):
                u = 4 * e + 2 * hf + q
                j = 2 * e + hf
                act.wait_ge(up1_ps, u + 1)
                wait(act, prod_set, u - 1)
                act.activation(sil[:, q, :], psum[:, 2 * q, :], ACT.Silu).then_inc(sil_set, 1)
                act.wait_ge(prod_set, u + 1)
                wait(act, down_ps, 2 * j - 2)
                act.activation(aT_hi[:, hf, q, :], prod[:, q, :], ACT.Copy).then_inc(ah_set, 1)

            unit(0, 0, 0)
            unit(0, 0, 1)
            act.wait_ge(logit_ps, 1)
            for hf in range(2):
                ins = act.activation(logT[:, hf * 512:(hf + 1) * 512], psum[0:2 * E, LOGT_BANK[hf], :], ACT.Copy)
            ins.then_inc(logT_set, 1)
            unit(0, 1, 0)
            act.wait_ge(lshift, 1)
            act.activation(expl[:, :, :], expl[:, :, :], ACT.Exp).then_inc(lexp, 1)
            unit(0, 1, 1)
            with act.Fori(1, E) as e:
                for hf in range(2):
                    for q in range(2):
                        unit(e, hf, q)

        @block.vector
        def _(dve):
            count = [0]

            def chain(ins):
                count[0] += 1
                ins.then_inc(pre_dve, 1)
                dve.wait_ge(pre_dve, count[0])

            dve.memset(ones[:, :], 1.0).then_inc(ones_set, 1)
            dve.memset(eps[:, :], EPS).then_inc(ones_set, 1)
            dve.memset(logit[:, :, E:E + 4], BIG).then_inc(ones_set, 1)
            dve.wait_ge(qemb_ps, 1)
            for k in range(KD):
                chain(dve.tensor_scalar(qemb[:, k, :], psum[:, 4, k * B:(k + 1) * B],
                                        sm[:, SMALL["b3"] + k:SMALL["b3"] + k + 1], 0.0, ALU.add, ALU.max))
            chain(dve.tensor_scalar(qs[:, :, :], qemb[:, :, :], float(S), None, ALU.mult))

            def cond_in_sum(b):
                tok = slice(b * S, (b + 1) * S)
                dve.wait_ge(xsum_set, b + 1)
                dve.tensor_tensor(vq[:, b, :], vsum[:, b, :], qemb[:, :, b], ALU.mult).then_inc(vq_set, 1)
                for k in range(KD):
                    ins = dve.tensor_scalar(xa[:, k, tok], xTs[:, k, tok], float(S), vsum[:, b, k:k + 1],
                                            ALU.mult, ALU.add)
                chain(ins)

            def cond_lo(b):
                tok = slice(b * S, (b + 1) * S)
                dve.wait_ge(xqh_set, b + 1)
                for k in range(KD):
                    ins = dve.scalar_tensor_tensor(out=actT_lo[:, k, tok], in0=xa[:, k, tok],
                                                   scalar=qemb[:, k, b:b + 1],
                                                   in1=actT_hi[:, k, tok].bitcast(F32),
                                                   op0=ALU.mult, op1=ALU.subtract)
                ins.then_inc(xql_set, 1)

            cond_in_sum(0)
            cond_in_sum(1)
            cond_lo(0)
            cond_in_sum(2)
            cond_lo(1)
            cond_in_sum(3)
            cond_lo(2)
            cond_lo(3)

            def normed(n):
                b = n % B
                c = (slice(None), n // B, slice(2 * b, 2 * b + 2))
                dve.wait_ge(sq_set, n + 1)
                dve.tensor_scalar(var[c], ss[c], 1.0 / D, EPS, ALU.mult, ALU.add)
                dve.wait_ge(std_set, n + 1)
                chain(dve.reciprocal(rstd[c], rstd[c]))
                chain(dve.scalar_tensor_tensor(out=nt1[c], in0=rstd[c], scalar=-0.5, in1=rstd[c],
                                               op0=ALU.mult, op1=ALU.mult))
                chain(dve.tensor_tensor(nt1[c], nt1[c], var[c], ALU.mult))
                chain(dve.scalar_tensor_tensor(out=rstd[c], in0=nt1[c], scalar=1.5, in1=rstd[c],
                                               op0=ALU.add, op1=ALU.mult))
                wait(dve, hnT_ps, n - 1)
                for t in range(2):
                    ins = dve.tensor_scalar(hn[:, n % 2, t, :], y[:, 2 * b + t, :],
                                            rstd[:, n // B, 2 * b + t:2 * b + t + 1], None, ALU.mult)
                ins.then_inc(hn_set, 1)

            def norm_lo(n):
                b = n % B
                tok = slice(b * S, (b + 1) * S)
                hi, lo = (hT_hi, hT_lo) if n < B else (actT_hi, actT_lo)
                w = SMALL["ln"] if n < B else SMALL["ffln"]
                dve.wait_ge(hh_set, n + 1)
                for k in range(KD):
                    ins = dve.scalar_tensor_tensor(out=lo[:, k, tok], in0=psum[:, NORM_BANK[n], k * S:(k + 1) * S],
                                                   scalar=sm[:, w + k:w + k + 1],
                                                   in1=hi[:, k, tok].bitcast(F32),
                                                   op0=ALU.mult, op1=ALU.subtract)
                ins.then_inc(hl_set, 1)

            normed(0)
            normed(1)
            norm_lo(0)
            normed(2)

            def columns(g, b, t):
                i = 4 * g + b
                dve.wait_ge(proj_ps, 2 * i + t + 1)
                if isinstance(g, int) and g == 0 and b == 0 and t == 0:
                    dve.wait_ge(rope_in, 16)
                wait(dve, rope_add, i)
                dve.tensor_tensor(rc[:, t, :], psum[:, PJ + t, 0:ROT], rope_sb[:, 0, t, :], ALU.mult)
                dve.tensor_tensor(rs_[:, t, :], psum[:, PJ + t, 0:ROT], rope_sb[:, 1, t, :], ALU.mult)\
                   .then_inc(rope_mul, 1)

            def values_lo(g, b):
                dve.wait_ge(vh_set, 4 * g + b + 1)
                for t in range(2):
                    ins = dve.tensor_tensor(v_lo[:, b, t, :, :],
                                            psum[:, PJ + t, None, ROT:QKV].to_broadcast([P, 2, HD]),
                                            v_hi[:, b, t, :, :].bitcast(F32), ALU.subtract)
                ins.then_inc(vl_set, 1)

            def qk_lo(g, b):
                dve.wait_ge(qkh_set, 4 * g + b + 1)
                dve.tensor_tensor(qT_lo[:, :, :], psum[:, QT, :].rearrange("p (a s) -> p a s", a=2),
                                  qT_hi[:, :, :].bitcast(F32), ALU.subtract)
                dve.tensor_tensor(kT_lo[:, :], psum[:, PJ, 0:S], kT_hi[:, :].bitcast(F32), ALU.subtract)\
                   .then_inc(qkl_set, 1)

            def maxima(g, b, p):
                m = 2 * (4 * g + b) + p
                dve.wait_ge(score_ps, m + 1)
                for t in range(2):
                    ins = dve.tensor_reduce(nmax[:, p, t, :],
                                            psum[:, S_BANK:S_BANK + 2, t * P:t * P + (t + 1) * P],
                                            X, ALU.max, negate=True)
                ins.then_inc(max_set, 1)

            def inverse(g, b, p):
                dve.wait_ge(exp_set, 2 * (4 * g + b) + p + 1)
                dve.reciprocal(rinv[:, p, :, :], rsum[:, p, :, :]).then_inc(inv_set, 1)

            def probT_lo(g, b, p):
                dve.wait_ge(pTh_set, 2 * (4 * g + b) + p + 1)
                dve.tensor_tensor(pT_lo[:, p, :, :], psum[:, PT_BANK:PT_BANK + 2, 0:3 * P],
                                  pT_hi[:, p, :, :].bitcast(F32), ALU.subtract).then_inc(pTl_set, 1)

            def value_lo(g, b, p):
                dve.wait_ge(oh_set, 2 * (4 * g + b) + p + 1)
                for h in range(2):
                    r = slice(h * HD, (h + 1) * HD)
                    ins = dve.tensor_tensor(oT_lo[r, b % 2, p, :], psum[r, PV, h * S:(h + 1) * S],
                                            oT_hi[r, b % 2, p, :].bitcast(F32), ALU.subtract)
                ins.then_inc(ol_set, 1)

            def residual(g, b):
                dve.wait_ge(wo_ps, 4 * g + b + 1)
                yb = y[:, 2 * b:2 * b + 2, :]
                dve.tensor_tensor(yb, psum[:, PJ + 1, :].rearrange("p (t d) -> p t d", t=2), yb, ALU.add)\
                   .then_inc(x1_set, 1)

            columns(0, 0, 0)
            columns(0, 0, 1)
            values_lo(0, 0)
            norm_lo(1)
            normed(3)
            qk_lo(0, 0)
            norm_lo(2)
            norm_lo(3)

            def step(g, b, has1, has2, more):
                nxt, prv = after(g, b), before(g, b)
                maxima(g, b, 0)
                if more:
                    columns(*nxt, 0)
                    columns(*nxt, 1)
                inverse(g, b, 0)
                if more:
                    values_lo(*nxt)
                if has1:
                    probT_lo(*prv, 1)
                    value_lo(*prv, 0)
                maxima(g, b, 1)
                if more:
                    qk_lo(*nxt)
                inverse(g, b, 1)
                if has2:
                    residual(*before(*prv))
                if has1:
                    value_lo(*prv, 1)
                probT_lo(g, b, 0)

            run_steps(dve, step)
            normed(4)
            probT_lo(KV - 1, B - 1, 1)
            value_lo(KV - 1, B - 1, 0)
            normed(5)
            residual(KV - 1, B - 2)
            norm_lo(4)
            value_lo(KV - 1, B - 1, 1)
            norm_lo(5)
            normed(6)
            residual(KV - 1, B - 1)
            normed(7)
            norm_lo(6)
            norm_lo(7)

            def shifted_logits():
                dve.wait_ge(logitT_ps, 1)
                lg = psum[:, LOGIT_BANK, 0:NT * 2 * E].rearrange("p (t a e) -> p t e a", t=NT, a=2)
                dve.tensor_reduce(logit[:, :, 0:E], lg, X, ALU.add).then_inc(logit_set, 1)
                dve.wait_ge(logit_set, 1)
                for tile in range(NT):
                    ins = dve.max(top[:, tile, :], logit[:, tile, 0:E])
                chain(ins)
                chain(dve.tensor_tensor(expl[:, :, :], logit[:, :, 0:E], top[:, :, 0:1].to_broadcast([P, NT, E]),
                                        ALU.subtract))
                dve.memset(top[:, :, TOPK:8], BIG).then_inc(lshift, 1)
                dve.wait_ge(lshift, 1)

            def choose():
                for tile in range(NT):
                    ins = dve.match_replace(left[:, tile, :], top[:, tile, :], logit[:, tile, :], -BIG)
                chain(ins)
                chain(dve.tensor_tensor(chosen[:, :, :], left[:, :, 0:E], logit[:, :, 0:E], ALU.not_equal))
                dve.wait_ge(lexp, 1)
                chain(dve.tensor_tensor(chosen[:, :, :], chosen[:, :, :], expl[:, :, :], ALU.mult))
                chain(dve.tensor_reduce(gsum[:, :], chosen[:, :, :], X, ALU.add))
                chain(dve.reciprocal(gsum[:, :], gsum[:, :]))
                chain(dve.tensor_tensor(gates[:, :, :], chosen[:, :, :],
                                        gsum[:, :, None].to_broadcast([P, NT, E]), ALU.mult))

            def product(e, hf, q):
                u = 4 * e + 2 * hf + q
                dve.wait_ge(sil_set, u + 1)
                dve.wait_ge(up3_ps, u + 1)
                wait(dve, ah_set, u - 1)
                dve.tensor_tensor(prod[:, q, :], psum[:, 2 * q + 1, :], sil[:, q, :], ALU.mult)\
                   .then_inc(prod_set, 1)
                dve.wait_ge(ah_set, u + 1)
                dve.tensor_tensor(aT_lo[:, hf, q, :], prod[:, q, :], aT_hi[:, hf, q, :].bitcast(F32),
                                  ALU.subtract).then_inc(al_set, 1)

            def accumulate(e, hf):
                j = 2 * e + hf
                for c in range(2):
                    dve.wait_ge(down_ps, 2 * j + c + 1)
                    for tt in range(2):
                        tile = 4 * hf + 2 * c + tt
                        ins = dve.scalar_tensor_tensor(out=y[:, tile, :],
                                                       in0=psum[:, 4 + 2 * hf + c, tt * D:(tt + 1) * D],
                                                       scalar=gates[:, tile, bass.ds(e, 1)], in1=y[:, tile, :],
                                                       op0=ALU.mult, op1=ALU.add)
                    ins.then_inc(acc_set, 1)

            def expert(e, first):
                for hf in range(2):
                    product(e, hf, 0)
                    if first and hf:
                        shifted_logits()
                    product(e, hf, 1)
                    if first and hf:
                        choose()
                        dve.wait_ge(xadd_set, 1)
                    if hf:
                        accumulate(e, 0)
                    elif not first:
                        accumulate(e - 1, 1)

            expert(0, True)
            with dve.Fori(1, E) as e:
                expert(e, False)
            accumulate(E - 1, 1)

        @block.gpsimd
        def _(pool):
            n_self = [0]

            def chain(ins):
                n_self[0] += 1
                ins.then_inc(pre_pool, 1)
                pool.wait_ge(pre_pool, n_self[0])

            def times_one(dst, src, shape):
                return pool.tensor_tensor(dst, src, ones[:, 0:1].to_broadcast(shape), ALU.mult)

            def split_proj_hi(g):
                pool.wait_ge(attw_in, 16 * (g + 1))
                if not isinstance(g, int) or g > 1:
                    pool.wait_ge(proj_ps, 8 * (g - 1))
                times_one(att_hi[:, g % 2, 0:WQ], att_raw[:, 0:WQ], [P, WQ]).then_inc(atth_set, 1)

            def split_proj_lo(g):
                pool.wait_ge(atth_set, 2 * g + 1)
                pool.tensor_tensor(att_lo[:, g % 2, 0:WQ], att_raw[:, 0:WQ], att_hi[:, g % 2, 0:WQ].bitcast(F32),
                                   ALU.subtract).then_inc(attw_split, 1)

            def split_out_hi(g):
                if not isinstance(g, int) or g > 1:
                    pool.wait_ge(wo_ps, 4 * (g - 1))
                times_one(att_hi[:, g % 2, WQ:], att_raw[:, WQ:], [P, WO]).then_inc(atth_set, 1)

            def split_out_lo(g):
                pool.wait_ge(atth_set, 2 * g + 2)
                pool.tensor_tensor(att_lo[:, g % 2, WQ:], att_raw[:, WQ:], att_hi[:, g % 2, WQ:].bitcast(F32),
                                   ALU.subtract).then_inc(attwo_split, 1)

            pool.wait_ge(ones_set, 1)
            def split(hi, lo, raw, ones_n, count):
                pool.tensor_tensor(hi, raw, ones_n, ALU.mult).then_inc(w2h_set, 1)
                pool.wait_ge(w2h_set, count)
                pool.tensor_tensor(lo, raw, hi.bitcast(F32), ALU.subtract).then_inc(w2_split, 1)

            pool.wait_ge(w2_in, 16)
            split(w2_hi[:, :, :], w2_lo[:, :, :], w2_raw[:, :, :], ones[:, 0:1, None].to_broadcast([P, KD, D]), 1)
            pool.wait_ge(b2_in, 32)
            pool.tensor_tensor(ones_r[:, :], ones[0:1, :], ones[0:1, :], ALU.mult)
            split(b2_parts[:, 0, :], b2_parts[:, 1, :], b2_sb[:, :], ones[0:1, 0:1].to_broadcast([1, 2 * D]), 2)
            split_proj_hi(0)
            split_proj_lo(0)
            split_out_hi(0)
            split_out_lo(0)
            wg = sm[:, SMALL["wg"]:SMALL["wg"] + KD * E].rearrange("p (k e) -> p k e", k=KD)
            pool.wait_ge(small_in, 16)
            chain(times_one(wg2[:, 0, 0, :], wg[:, 0, :], [P, E]))
            chain(times_one(wg2[:, 1, 0, :], wg[:, 1, :], [P, E]))
            chain(pool.tensor_tensor(wg2[:, :, 1, :], wg, wg2[:, :, 0, :].bitcast(F32), ALU.subtract))

            def rope(g, b):
                i = 4 * g + b
                wait(pool, qkT_ps, i)
                c = rc[:, :, :].rearrange("p t (h a e) -> p t h a e", a=2, e=HD // 2)
                s = rs_[:, :, :].rearrange("p t (h a e) -> p t h a e", a=2, e=HD // 2)
                r = rot[:, :, :].rearrange("p t (h a e) -> p t h a e", a=2, e=HD // 2)
                for t in range(2):
                    pool.wait_ge(rope_mul, 2 * i + t + 1)
                    for a in range(2):
                        pool.tensor_tensor(r[:, t, 0:GH + 1, a, :], c[:, t, :, a, :], s[:, t, :, 1 - a, :], ALU.add)
                for a in range(2):
                    ins = pool.tensor_tensor(r[:, :, GH + 1, a, :], c[:, :, GH, a, :], s[:, :, GH, 1 - a, :],
                                             ALU.add)
                ins.then_inc(rope_add, 1)

            def normalise(g, b, p):
                pool.wait_ge(inv_set, 2 * (4 * g + b) + p + 1)
                for t in range(2):
                    w = (t + 1) * P
                    pr = prob[:, p, :, t * P:t * P + w]
                    ins = pool.tensor_tensor(pr, pr, rinv[:, p, t, :, None].to_broadcast([P, 2, w]), ALU.mult)
                ins.then_inc(norm_set, 1)

            rope(0, 0)

            def step(g, b, has1, has2, more):
                if more:
                    rope(*after(g, b))
                normalise(g, b, 0)
                normalise(g, b, 1)
                if isinstance(g, int) and g == KV - 1:
                    if b % 2 == 0:
                        exp_split_hi(b // 2, b // 2)
                    else:
                        exp_split_lo(b // 2, b // 2)
                elif b == 0:
                    split_proj_hi(g + 1)
                elif b == 1:
                    split_proj_lo(g + 1)
                elif b == 2:
                    split_out_hi(g + 1)
                else:
                    split_out_lo(g + 1)

            def exp_split_hi(e, par):
                pool.wait_ge(expw_in[par], 16 * (e // 2 + 1) if isinstance(e, int) else 8 * (e - par) + 16)
                wait(pool, down_ps, 4 * (e - 1))
                times_one(exp_hi[:, par, :], exp_raw[:, par, :], [P, EW]).then_inc(exph_set, 1)

            def exp_split_lo(e, par):
                pool.wait_ge(exph_set, e + 1)
                pool.tensor_tensor(exp_lo[:, par, :], exp_raw[:, par, :], exp_hi[:, par, :].bitcast(F32),
                                   ALU.subtract).then_inc(expw_split, 1)

            run_steps(pool, step)
            pool.wait_ge(xn_in, 16)
            pool.wait_ge(hn_set, 2 * B)
            pool.tensor_tensor(y[:, :, :], y[:, :, :], x_sb[:, :, :], ALU.add).then_inc(xadd_set, 1)
            with pool.Fori(1, E // 2) as ep:
                for par in range(2):
                    exp_split_hi(2 * ep + par, par)
                    exp_split_lo(2 * ep + par, par)


def kernel(x, cond_1024, L0_cond_W3, L0_cond_b3, L0_cond_W2, L0_cond_b2, L0_ffn_ln_w, L0_ffn_ff_ln_w,
           L0_ffn_wq, L0_ffn_wk, L0_ffn_wv, L0_ffn_wo, L0_ffn_wg, L0_ffn_w1, L0_ffn_w3, L0_ffn_w2):
    import ml_dtypes
    import concourse.bacc as _bacc
    from concourse.bass_utils import run_bass_kernel_spmd as _run

    def a(v):
        return np.asarray(v)

    def cols(v):
        return a(v).reshape(KD, P).T

    def rows(w):
        w = a(w)
        return w.reshape(-1, P, w.shape[-1]).transpose(1, 0, 2)

    xf = a(x).reshape(B * S, D)
    small = np.concatenate([a(cond_1024).T, cols(L0_cond_b3), cols(L0_ffn_ln_w), cols(L0_ffn_ff_ln_w),
                            rows(L0_ffn_wg).reshape(P, KD * E), np.eye(P, dtype=np.float32)], axis=1)
    wq = rows(L0_ffn_wq).reshape(P, KD, KV, GH * HD)
    wk = rows(L0_ffn_wk).reshape(P, KD, KV, HD)
    wv = rows(L0_ffn_wv).reshape(P, KD, KV, HD)
    qkv = np.concatenate([wq, wk, wv], axis=3).transpose(2, 0, 1, 3).reshape(KV, P, WQ)
    wo = a(L0_ffn_wo).reshape(KV, 2, P, D).transpose(0, 2, 1, 3).reshape(KV, P, WO)
    attw = np.concatenate([qkv, wo], axis=2)
    expw = np.stack([a(w).reshape(E, KD, P, D).transpose(0, 2, 1, 3) for w in (L0_ffn_w1, L0_ffn_w3, L0_ffn_w2)],
                    axis=2).reshape(E, P, EW)
    half = HD // 2
    inv = (np.float32(1.0) / np.float32(150000.0) ** (np.arange(half, dtype=np.float32) / np.float32(half)))
    ang = np.arange(S, dtype=np.float32)[:, None] * inv.astype(np.float32)
    cos, sin = np.cos(ang), np.sin(ang)
    scale = np.array([HD ** -0.5] * GH + [1.0], np.float32)[None, :, None, None]
    tab = np.stack([np.stack([cos, cos], 1)[:, None] * scale, np.stack([sin, -sin], 1)[:, None] * scale])
    rope = tab.astype(np.float32).reshape(2, 2, P, ROT).transpose(2, 0, 1, 3)
    mask = np.triu(np.full((P, P), -1e30, np.float32), 1).astype(ml_dtypes.bfloat16)

    data = dict(small=small, w3=a(L0_cond_W3), w2c=a(L0_cond_W2), b2=a(L0_cond_b2).reshape(1, D), xT=xf.T,
                xn=xf, rope=rope, mask=mask, attw=attw, expw=expw)
    nc = _bacc.Bacc("TRN2", target_bir_lowering=False, num_devices=1)
    arrays, args = {}, {}
    for name, v in data.items():
        v = np.ascontiguousarray(v)
        arrays["in_" + name] = v
        args[name] = nc.dram_tensor("in_" + name, v.shape, mybir.dt.from_np(v.dtype), kind="ExternalInput").ap()
    res = nc.dram_tensor("res", (B * S, D), F32, kind="ExternalOutput").ap()
    build(nc, out=res, **args)
    r = _run(nc, [arrays], core_ids=[0])
    return r.results[0]["res"].reshape(B, S, D)
```
